# Optimizing a Trainium2 kernel written in Bass

```python
import numpy as np
import jax
import jax.numpy as jnp

def _softmax(x, axis=-1):
    return jax.nn.softmax(x, axis=axis)

def _gelu(x):
    return jax.nn.gelu(x, approximate=True)

def _silu(x):
    return jax.nn.silu(x)

def _sigmoid(x):
    return jax.nn.sigmoid(x)

def _layernorm(x, axis=-1, eps=1e-05):
    m = jnp.mean(x, axis=axis, keepdims=True)
    v = jnp.var(x, axis=axis, keepdims=True)
    return (x - m) / jnp.sqrt(v + eps)

def _scatter_add(tgt, idx, src, axis=0):
    return tgt.at[idx].add(src)

def _segment_sum(src, seg, n):
    return jax.ops.segment_sum(src, seg, n)
kernel_name = 'mk_seq_preln_d1_jaxref_r8_be47e3'

def setup_inputs(seed: int=0):
    np.random.seed(seed)
    _w = jnp.asarray

    def _L0_attn_setup():
        import jax, jax.numpy as jnp
        import numpy as np
        INDIM = 128
        NHEADS = 16
        DK = INDIM // NHEADS
        DV = INDIM // NHEADS
        B, S = (4, 256)
        key = jax.random.key(seed)
        ks = jax.random.split(key, 5)
        x = jax.random.normal(ks[0], (B, S, INDIM), dtype=jnp.float32)
        std_qk = np.sqrt(2.0 / (INDIM + DK)).astype(np.float32)
        std_v = np.sqrt(2.0 / (INDIM + DV)).astype(np.float32)
        Wq = jax.random.normal(ks[1], (NHEADS * DK, INDIM), dtype=jnp.float32) * std_qk
        Wk = jax.random.normal(ks[2], (NHEADS * DK, INDIM), dtype=jnp.float32) * std_qk
        Wv = jax.random.normal(ks[3], (NHEADS * DV, INDIM), dtype=jnp.float32) * std_v
        std_o = np.sqrt(2.0 / (NHEADS * DV + INDIM)).astype(np.float32)
        Wo = jax.random.normal(ks[4], (INDIM, NHEADS * DV), dtype=jnp.float32) * std_o
        bq = jnp.zeros((NHEADS * DK,), jnp.float32)
        bk = jnp.zeros((NHEADS * DK,), jnp.float32)
        bv = jnp.zeros((NHEADS * DV,), jnp.float32)
        bo = jnp.zeros((INDIM,), jnp.float32)
        return {'x': x, 'Wq': Wq, 'bq': bq, 'Wk': Wk, 'bk': bk, 'Wv': Wv, 'bv': bv, 'Wo': Wo, 'bo': bo}
    _L0_attn_in = _L0_attn_setup()

    def _L0_ffn_setup():
        import jax, jax.numpy as jnp
        import numpy as np
        import math
        DIM = 128
        NUM_HEADS = 16
        SHARED_HEADS = 1
        ROUTED_HEADS = 3
        HEAD_DIM = DIM // NUM_HEADS
        B, N = (2, 256)
        key = jax.random.key(seed)
        ks = jax.random.split(key, 16)
        s = 1.0 / math.sqrt(DIM)
        inp = {'x': jax.random.normal(ks[0], (B, N, DIM), dtype=jnp.float32), 'Wq': jax.random.uniform(ks[1], (DIM, DIM), minval=-s, maxval=s), 'bq': jax.random.uniform(ks[2], (DIM,), minval=-s, maxval=s), 'Wk': jax.random.uniform(ks[3], (DIM, DIM), minval=-s, maxval=s), 'bk': jax.random.uniform(ks[4], (DIM,), minval=-s, maxval=s), 'Wv': jax.random.uniform(ks[5], (DIM, DIM), minval=-s, maxval=s), 'bv': jax.random.uniform(ks[6], (DIM,), minval=-s, maxval=s), 'Wp': jax.random.uniform(ks[7], (DIM, DIM), minval=-s, maxval=s), 'bp': jax.random.uniform(ks[8], (DIM,), minval=-s, maxval=s), 'Wr': jax.random.uniform(ks[9], (NUM_HEADS - SHARED_HEADS, DIM), minval=-s, maxval=s), 'br': jax.random.uniform(ks[10], (NUM_HEADS - SHARED_HEADS,), minval=-s, maxval=s), 'Ws': jax.random.uniform(ks[11], (2, DIM), minval=-s, maxval=s), 'bs': jax.random.uniform(ks[12], (2,), minval=-s, maxval=s), 'temperature': jnp.full((NUM_HEADS, 1, 1), float(np.log(np.expm1(1.0 / 0.24))), dtype=jnp.float32), 'query_embedding': 0.02 * jax.random.normal(ks[13], (NUM_HEADS, 1, HEAD_DIM), dtype=jnp.float32)}
        return inp
    _L0_ffn_in = _L0_ffn_setup()
    _d = {'L0_attn_x': _L0_attn_in['x'], 'L0_attn_Wq': _L0_attn_in['Wq'], 'L0_attn_bq': _L0_attn_in['bq'], 'L0_attn_Wk': _L0_attn_in['Wk'], 'L0_attn_bk': _L0_attn_in['bk'], 'L0_attn_Wv': _L0_attn_in['Wv'], 'L0_attn_bv': _L0_attn_in['bv'], 'L0_attn_Wo': _L0_attn_in['Wo'], 'L0_attn_bo': _L0_attn_in['bo'], 'L0_ffn_Wq': _L0_ffn_in['Wq'], 'L0_ffn_bq': _L0_ffn_in['bq'], 'L0_ffn_Wk': _L0_ffn_in['Wk'], 'L0_ffn_bk': _L0_ffn_in['bk'], 'L0_ffn_Wv': _L0_ffn_in['Wv'], 'L0_ffn_bv': _L0_ffn_in['bv'], 'L0_ffn_Wp': _L0_ffn_in['Wp'], 'L0_ffn_bp': _L0_ffn_in['bp'], 'L0_ffn_Wr': _L0_ffn_in['Wr'], 'L0_ffn_br': _L0_ffn_in['br'], 'L0_ffn_Ws': _L0_ffn_in['Ws'], 'L0_ffn_bs': _L0_ffn_in['bs'], 'L0_ffn_temperature': _L0_ffn_in['temperature'], 'L0_ffn_query_embedding': _L0_ffn_in['query_embedding']}
    _x0 = _d['L0_attn_x']
    _d['L0_attn_x'] = jax.random.normal(jax.random.fold_in(jax.random.key(seed), 1), (2, 1024, 128), dtype=_x0.dtype)
    del _x0
    return _d

def reference(L0_attn_x, L0_attn_Wq, L0_attn_bq, L0_attn_Wk, L0_attn_bk, L0_attn_Wv, L0_attn_bv, L0_attn_Wo, L0_attn_bo, L0_ffn_Wq, L0_ffn_bq, L0_ffn_Wk, L0_ffn_bk, L0_ffn_Wv, L0_ffn_bv, L0_ffn_Wp, L0_ffn_bp, L0_ffn_Wr, L0_ffn_br, L0_ffn_Ws, L0_ffn_bs, L0_ffn_temperature, L0_ffn_query_embedding):

    def _L0_attn_ref(x, Wq, bq, Wk, bk, Wv, bv, Wo, bo):
        import jax, jax.numpy as jnp
        import numpy as np
        INDIM = 128
        NHEADS = 16
        DK = INDIM // NHEADS
        DV = INDIM // NHEADS
        B, S = (4, 256)
        b, s, _ = x.shape
        q = (x @ Wq.T + bq).reshape(b, s, NHEADS, DK)
        k = (x @ Wk.T + bk).reshape(b, s, NHEADS, DK)
        v = (x @ Wv.T + bv).reshape(b, s, NHEADS, DV)
        w = jnp.einsum('bshd,bzhd->bhsz', q, k)
        w = w / jnp.sqrt(jnp.float32(DV))
        w = jax.nn.softmax(w, axis=-1)
        vw = jnp.einsum('bhsz,bzhd->bshd', w, v)
        vw = vw.reshape(b, s, NHEADS * DV)
        out = vw @ Wo.T + bo
        return out

    def _L0_ffn_ref(x, Wq, bq, Wk, bk, Wv, bv, Wp, bp, Wr, br, Ws, bs, temperature, query_embedding):
        import jax, jax.numpy as jnp
        import numpy as np
        import math
        DIM = 128
        NUM_HEADS = 16
        SHARED_HEADS = 1
        ROUTED_HEADS = 3
        HEAD_DIM = DIM // NUM_HEADS
        B, N = (2, 256)
        Bsz, Nn, C = x.shape
        H, hd = (NUM_HEADS, HEAD_DIM)

        def heads(W, b):
            y = x @ W.T + b
            return y.reshape(Bsz, Nn, H, hd).transpose(0, 2, 1, 3)
        q = heads(Wq, bq)
        k = heads(Wk, bk)
        v = heads(Wv, bv)
        q_norm = q / jnp.linalg.norm(q, axis=-1, keepdims=True)
        q_scaled = (q_norm + query_embedding[None]) * jax.nn.softplus(temperature)[None]
        attn = jnp.einsum('bhqd,bhkd->bhqk', q_scaled, k) / math.sqrt(hd)
        attn = jax.nn.softmax(attn, axis=-1)
        h = jnp.einsum('bhqk,bhkd->bhqd', attn, v)
        h = h.transpose(0, 2, 1, 3).reshape(Bsz, Nn, C)
        gates = jax.nn.softmax(h @ Wr.T + br, axis=-1)
        _, idx = jax.lax.top_k(gates, ROUTED_HEADS)
        mask = jax.nn.one_hot(idx, H - SHARED_HEADS, dtype=gates.dtype).sum(axis=-2)
        routed_gates = gates * mask * ROUTED_HEADS
        sw = jax.nn.softmax(h @ Ws.T + bs, axis=-1)
        shared_gates = sw * SHARED_HEADS
        weight_0 = sw * 2.0
        shared_gates = weight_0[..., 0:1] * shared_gates
        routed_gates = weight_0[..., 1:2] * routed_gates
        masked_gates = jnp.concatenate([shared_gates, routed_gates], axis=-1)
        out = h * masked_gates.sum(axis=-1, keepdims=True)
        return out @ Wp.T + bp
    x = L0_attn_x
    x = x + _L0_attn_ref(_layernorm(x, axis=-1), L0_attn_Wq, L0_attn_bq, L0_attn_Wk, L0_attn_bk, L0_attn_Wv, L0_attn_bv, L0_attn_Wo, L0_attn_bo)
    x = x + _L0_ffn_ref(_layernorm(x, axis=-1), L0_ffn_Wq, L0_ffn_bq, L0_ffn_Wk, L0_ffn_bk, L0_ffn_Wv, L0_ffn_bv, L0_ffn_Wp, L0_ffn_bp, L0_ffn_Wr, L0_ffn_br, L0_ffn_Ws, L0_ffn_bs, L0_ffn_temperature, L0_ffn_query_embedding)
    return x

_drawn_inputs = setup_inputs


def setup_inputs(seed=0):
    import zlib

    import numpy as np

    out = dict(_drawn_inputs(seed))
    spreads = {'L0_attn_bq': (0.0, 0.315),
     'L0_attn_bk': (0.0, 2.0),
     'L0_attn_bv': (0.0, 0.1),
     'L0_attn_bo': (0.0, 0.1),
     'L0_ffn_temperature': (4.151041507720947, 0.6)}
    factors = {'L0_ffn_bq': 8.0,
     'L0_ffn_bk': 64.0,
     'L0_ffn_Wr': 29.674,
     'L0_ffn_br': 42.551,
     'L0_ffn_Ws': 8.0,
     'L0_ffn_bs': 64.0,
     'L0_ffn_query_embedding': 8.0}
    for name, (base, spread) in spreads.items():
        noise = np.random.default_rng([zlib.crc32(name.encode()), seed]).standard_normal(out[name].shape)
        drawn = base * np.exp(spread * noise) if base else spread * noise
        out[name] = jnp.asarray(drawn.astype(out[name].dtype))
    for name, factor in factors.items():
        out[name] = (out[name] * factor).astype(out[name].dtype)
    return out
```

```python
import concourse.bass as bass
from concourse import mybir
from contextlib import ExitStack

F32 = mybir.dt.float32
BF16 = mybir.dt.bfloat16
ALU = mybir.AluOpType
ACT = mybir.ActivationFunctionType
AX = mybir.AxisListType

B, S, D, H = 2, 1024, 128, 16
DH = D // H
TILES = S // 128
HALF = 512
PAIRS = H // 2
SEGMENTS = 2 * B
ALL_PAIRS = SEGMENTS * PAIRS
NG = H - 1
TOP = 3
EPS = 1e-5

Q_PART = [0, 0, 1, 0, 2, 1]
K_PART = [0, 1, 0, 2, 0, 1]
COMBOS = len(Q_PART)
CROWS = COMBOS * DH
SROWS = CROWS + 2
MROWS = 3 * DH
VROW = DH + 1
VPAIR = 2 * TILES * VROW
AHEAD = 3

W_COLS = {}
_at = 0
for _name, _n in (("q1", D), ("k1", D), ("v1", D), ("o1", D), ("q2", D), ("k2", D), ("v2", D),
                  ("p2", D + NG + 2), ("ident", D), ("same_head", D)):
    W_COLS[_name] = (_at, _at + _n)
    _at += _n
W_WIDTH = _at
COLS = ["bq1", "bk1", "bq2", "bk2", "qe", "temp"]
R_COLS = {}
_at = 0
for _name, _n in (("bv1", D), ("bo1", D), ("bv2", D), ("bp", D), ("brs", NG + 2)):
    R_COLS[_name] = (_at, _at + _n)
    _at += _n
R_WIDTH = _at
OUTW = D + NG + 2


def moe_attention_program(nc, x, wmat, wcol, wrow, out, qc, kc, os_):
    ctx = ExitStack()
    with ctx:
        def sb(name, shape, dt=F32):
            return ctx.enter_context(nc.sbuf_tensor(name, shape, dt))

        def sem(name):
            return ctx.enter_context(nc.semaphore(name))

        X = sb("X", [128, B, TILES, D])
        W = sb("W", [128, W_WIDTH])
        C = sb("C", [128, len(COLS)])
        R = sb("R", [128, R_WIDTH])
        col = {n: C[:, i:i + 1] for i, n in enumerate(COLS)}
        w = {n: W[:, a:b] for n, (a, b) in W_COLS.items()}
        row = {n: R[:, a:b] for n, (a, b) in R_COLS.items()}
        qbias = sb("qbias", [128, 1])
        head_scale = sb("head_scale", [128, 1])
        soft = sb("soft", [128, 3])
        stats = sb("stats", [128, TILES, 6])
        mv = sb("mv", [128, TILES, 2])
        var = sb("var", [128, TILES])
        lnv = sb("lnv", [128, TILES])
        rs0 = sb("rs0", [128, TILES])
        rst = sb("rst", [128, TILES])
        rstd = sb("rstd", [128, TILES])
        XN = sb("XN", [128, TILES, D])
        XNT = sb("XNT", [128, S])
        QT = sb("QT", [128, S])
        KT = sb("KT", [128, S])
        QR = sb("QR", [128, S])
        QB = sb("QB", [128, 3, S], BF16)
        KB = sb("KB", [128, 3, S], BF16)
        SQ = sb("SQ", [128, S])
        N2 = sb("N2", [128, S])
        LN2 = sb("LN2", [128, S])
        Y = sb("Y", [128, S])
        VA = sb("VA", [128, ALL_PAIRS, VPAIR])
        STQ = sb("STQ", [128, 2, 2, S], BF16)
        STK = sb("STK", [128, 2, S], BF16)
        MXQ = sb("MXQ", [128, 2, 2, S], BF16)
        MXK = sb("MXK", [128, 2, S], BF16)
        VR = sb("VR", [128, 2, VPAIR])
        NM = sb("NM", [128, 2, 2 * TILES])
        NB = sb("NB", [2 * TILES, 2, 2, 128], BF16)
        PT = sb("PT", [128, 2, 4, HALF])
        E = sb("E", [128, 2, HALF])
        ON = sb("ON", [128, S])
        DEN = sb("DEN", [128, S])
        RDEN = sb("RDEN", [128, S])
        ONN = sb("ONN", [128, S])
        Z = sb("Z", [128, TILES, OUTW])
        GL = sb("GL", [128, TILES, NG + 2])
        GE = sb("GE", [128, TILES, NG + 2])
        GM = sb("GM", [128, 2, TILES])
        T8 = sb("T8", [128, TILES, 8])
        GS = sb("GS", [128, 2, TILES])
        GR = sb("GR", [128, 2, TILES])
        G3 = sb("G3", [128, 3, TILES])
        SW = sb("SW", [128, TILES, 2])
        gate = sb("gate", [128, TILES])

        ST = ctx.enter_context(nc.psum_tensor("ST", [128, 2, HALF], F32))
        MX = ctx.enter_context(nc.psum_tensor("MX", [128, 2, 2 * HALF], F32))
        PV = ctx.enter_context(nc.psum_tensor("PV", [128, HALF], F32))
        XB = ctx.enter_context(nc.psum_tensor("XB", [128, HALF], F32))
        bank = [ST[:, 0, :], ST[:, 1, :], XB[:, :]]

        x_loaded = [sem(f"x_loaded{b}") for b in range(B)]
        w_loaded = sem("w_loaded")
        ones_ready = sem("ones_ready")
        fill_ready = sem("fill_ready")
        small_act = sem("small_act")
        small_ready = sem("small_ready")
        ld_mx = [sem(f"ld_mx{u}") for u in range(2)]
        ld_st = [sem(f"ld_st{u}") for u in range(2)]
        ld_m = [sem(f"ld_m{u}") for u in range(2)]
        st_ready, exp_done = sem("st_ready"), sem("exp_done")
        mx_ready, mx_taken = sem("mx_ready"), sem("mx_taken")
        mt_ready, nm_first, nm_ready = sem("mt_ready"), sem("nm_first"), sem("nm_ready")
        pv_done, evac = sem("pv_done"), sem("evac")
        e_store = [sem(f"e_store{u}") for u in range(2)]
        ln_dve, var_ready, rs_act, xn_ready = sem("ln_dve"), sem("var_ready"), sem("rs_act"), sem("xn_ready")
        c_ready, c_act, c_dve = sem("c_ready"), sem("c_act"), sem("c_dve")
        sq_ready, n_ready, n_act = sem("sq_ready"), sem("n_ready"), sem("n_act")
        pool1, pool2 = sem("pool1"), sem("pool2")
        parts_stored = sem("parts_stored")
        on_loaded, e_dve, on_ready = sem("on_loaded"), sem("e_dve"), sem("on_ready")
        biased, e_done = sem("biased"), sem("e_done")
        y_ready, y_taken = sem("y_ready"), sem("y_taken")
        z_ready, z_taken = sem("z_ready"), sem("z_taken")
        g_dve, g_act, out_ready, out_stored = sem("g_dve"), sem("g_act"), sem("out_ready"), sem("out_stored")

        G_STEPS, G_BEFORE = 18, 5
        block = ctx.enter_context(nc.Block())

        def wait(eng, s, value):
            if not isinstance(value, int) or value > 0:
                eng.wait_ge(s, value)

        @block.sync
        def _(sp):
            for b in range(B):
                sp.dma_start(X[:, b], x[b * S:(b + 1) * S].rearrange("(t p) c -> p t c", p=128))\
                  .then_inc(x_loaded[b], 16)
                if b == 0:
                    sp.dma_start(W[:, :], wmat).then_inc(w_loaded, 16)
                    sp.dma_start(C[:, :], wcol).then_inc(w_loaded, 16)
                    sp.dma_start(R[:, :], wrow.to_broadcast([128, R_WIDTH])).then_inc(w_loaded, 16)

            def load_max(p, u):
                for hh in range(2):
                    rows = slice(64 * hh, 64 * hh + MROWS)
                    sp.dma_start(MXQ[rows, u, hh, :], qc[bass.ds(2 * p + hh, 1), 0:MROWS, :]).then_inc(ld_mx[u], 16)
                    sp.dma_start(MXK[rows, u, :], kc[bass.ds(2 * p + hh, 1), 0:MROWS, :]).then_inc(ld_mx[u], 16)

            def load_scores(p, u):
                for hh in range(2):
                    sp.dma_start(STQ[64 * hh:64 * hh + CROWS, u, hh, :], qc[bass.ds(2 * p + hh, 1)])\
                      .then_inc(ld_st[u], 16)
                    sp.dma_start(STK[64 * hh:64 * hh + CROWS, u, :], kc[bass.ds(2 * p + hh, 1)])\
                      .then_inc(ld_st[u], 16)
                sp.dma_start(VR[:, u, :], VA[:, bass.ds(p, 1), :]).then_inc(ld_st[u], 16)

            def load_shift(u):
                for hh in range(2):
                    for part in range(2):
                        r = 64 * hh + CROWS + part
                        sp.dma_start(STQ[r:r + 1, u, hh, :], NB[TILES * hh:TILES * (hh + 1), u, part, :])\
                          .then_inc(ld_m[u], 16)

            def store_result(p, u):
                for hh in range(2):
                    for qh in range(2):
                        g = 2 * hh + qh
                        sp.dma_start(os_[bass.ds(2 * p + hh, 1), qh], E[32 * g:32 * g + VROW, u, :])\
                          .then_inc(e_store[u], 16)

            def pair(p, u, first=False, left=3):
                if left >= 1:
                    if not first:
                        sp.wait_ge(pv_done, TILES * p)
                    load_scores(p + 1, 1 - u)
                if not first:
                    sp.wait_ge(evac, p)
                    store_result(p - 1, 1 - u)
                if left >= 3:
                    sp.wait_ge(mx_ready, 2 * TILES * (p + 2))
                    load_max(p + 3, 1 - u)
                if left >= 1:
                    sp.wait_ge(nm_ready, p + 2)
                    load_shift(1 - u)

            sp.wait_ge(fill_ready, 4)
            sp.wait_ge(parts_stored, 2 * COMBOS * 16)
            load_max(0, 0)
            load_max(1, 1)
            sp.wait_ge(c_dve, 5)
            load_scores(0, 0)
            sp.wait_ge(nm_ready, 1)
            load_shift(0)
            sp.wait_ge(mx_ready, 2 * TILES)
            load_max(2, 0)
            pair(0, 0, first=True)
            with sp.Fori(0, 2) as k:
                pair(2 * k + 1, 1)
                pair(2 * k + 2, 0)
            for g in range(SEGMENTS - 1):
                sp.wait_ge(parts_stored, 2 * COMBOS * 16 * g + 2 * 2 * COMBOS * 16)
                sp.wait_ge(c_dve, 5 * g + 10)
                with sp.Fori(4 * g + 2, 4 * g + 6) as k:
                    pair(2 * k + 1, 1)
                    pair(2 * k + 2, 0)
            for left in (2, 1, 0):
                p = ALL_PAIRS - 1 - left
                pair(p, p % 2, left=left)
            sp.wait_ge(evac, ALL_PAIRS)
            store_result(ALL_PAIRS - 1, 1)
            for b in range(B):
                sp.wait_ge(out_ready, b + 1)
                sp.dma_start(out[b * S:(b + 1) * S].rearrange("(t p) c -> p t c", p=128), X[:, b])\
                  .then_inc(out_stored, 16)
            sp.wait_ge(out_stored, 16 * B)
            sp.wait_ge(parts_stored, SEGMENTS * 2 * COMBOS * 16)
            for u in range(2):
                sp.wait_ge(e_store[u], ALL_PAIRS // 2 * 64)

        @block.tensor
        def _(pe):
            def maxima(pm, u, qt, loaded=None):
                if loaded is not None:
                    pe.wait_ge(ld_mx[u], loaded)
                for hh in range(2):
                    wait(pe, mx_taken, 2 * TILES * pm + 2 * qt + hh - 1)
                    for kh in range(2):
                        here = slice(kh * HALF, (kh + 1) * HALF)
                        last = nc.tensor.matmul(MX[:, hh, here], MXQ[:, u, hh, qt * 128:(qt + 1) * 128],
                                                MXK[:, u, here], start=True, stop=True)
                    last.then_inc(mx_ready, 1)

            def turn_maxima(pm, u):
                pe.wait_ge(mx_taken, 2 * TILES * pm + 2 * TILES)
                wait(pe, nm_ready, pm)
                nc.tensor.transpose(XB[0:2 * TILES, 0:128], NM[:, u, :], w["ident"]).then_inc(mt_ready, 1)

            def scores(p, u, s, half):
                for hh in range(2):
                    j = 2 * half + hh
                    n = 4 * TILES * p + 4 * s + j
                    wait(pe, exp_done, n - 1)
                    nc.tensor.matmul(ST[:, j % 2, :], STK[:, u, s * 128:(s + 1) * 128],
                                     STQ[:, u, hh, half * HALF:(half + 1) * HALF],
                                     start=True, stop=True).then_inc(st_ready, 1)

            def values(p, u, s):
                pe.wait_ge(exp_done, 4 * TILES * p + 4 * s + 4)
                if s == 0:
                    wait(pe, evac, p)
                for j in range(4):
                    half, hh = j // 2, j % 2
                    g = 2 * hh + half
                    v = (hh * TILES + s) * VROW
                    last = nc.tensor.matmul(PV[32 * g:32 * g + VROW, :], VR[:, u, v:v + VROW],
                                            PT[:, s % 2, j, :], start=(s == 0), stop=(s == TILES - 1))
                last.then_inc(pv_done, 1)

            def pair(p, u, it, first=False, left=2):
                pe.wait_ge(ld_st[u], 80 * it + 80)
                pe.wait_ge(ld_m[u], 64 * it + 64)
                for s in range(TILES):
                    scores(p, u, s, 0)
                    if s < TILES - AHEAD:
                        if left >= 1:
                            maxima(p + 1, 1 - u, s + AHEAD)
                    elif left >= 2:
                        maxima(p + 2, u, s - (TILES - AHEAD),
                               64 * it + 128 if s == TILES - AHEAD else None)
                    scores(p, u, s, 1)
                    if s == TILES - 2 and left >= 1:
                        turn_maxima(p + 1, 1 - u)
                    if s > 0:
                        values(p, u, s - 1)
                    elif not first:
                        values(p - 1, 1 - u, TILES - 1)

            def body(it, first=False, last=False):
                pair(2 * it, 0, it, first, left=1 if last else 2)
                pair(2 * it + 1, 1, it, left=0 if last else 2)

            def settled(pairs):
                wait(pe, exp_done, 4 * TILES * pairs)
                wait(pe, nm_ready, 0 if isinstance(pairs, int) and pairs == 0 else pairs + 1)

            def project(g, layer, pairs):
                settled(pairs)
                pe.wait_ge(xn_ready, g + 1)
                for t in range(TILES):
                    last = nc.tensor.transpose(bank[t // 4][:, t % 4 * 128:(t % 4 + 1) * 128], XN[:, t, :],
                                               w["ident"])
                    if t % 4 == 3:
                        last.then_inc(c_ready, 1)
                pe.wait_ge(c_act, 3 * g + 1)
                nc.tensor.matmul(bank[2], w[f"q{layer}"], XNT[:, 0:HALF], start=True, stop=True)\
                  .then_inc(c_ready, 1)
                pe.wait_ge(c_dve, 5 * g + 1)
                nc.tensor.matmul(bank[0], w[f"q{layer}"], XNT[:, HALF:S], start=True, stop=True)\
                  .then_inc(c_ready, 1)
                nc.tensor.matmul(bank[1], w[f"k{layer}"], XNT[:, 0:HALF], start=True, stop=True)\
                  .then_inc(c_ready, 1)
                pe.wait_ge(c_act, 3 * g + 2)
                nc.tensor.matmul(bank[2], w[f"k{layer}"], XNT[:, HALF:S], start=True, stop=True)\
                  .then_inc(c_ready, 1)
                for n in range(2):
                    if n == 0:
                        pe.wait_ge(c_act, 3 * g + 3)
                    else:
                        pe.wait_ge(c_dve, 5 * g + 2)
                    for t in range(4):
                        k = 4 * n + t
                        last = nc.tensor.matmul(bank[n][:, t * 128:(t + 1) * 128],
                                                XNT[:, k * 128:(k + 1) * 128], w[f"v{layer}"],
                                                start=True, stop=True)
                    last.then_inc(c_ready, 1)
                if layer == 2:
                    pe.wait_ge(c_dve, 5 * g + 3)
                    pe.wait_ge(sq_ready, g - 1)
                    nc.tensor.matmul(bank[2], w["same_head"], SQ[:, 0:HALF], start=True, stop=True)\
                      .then_inc(n_ready, 1)
                    pe.wait_ge(c_dve, 5 * g + 4)
                    nc.tensor.matmul(bank[0], w["same_head"], SQ[:, HALF:S], start=True, stop=True)\
                      .then_inc(n_ready, 1)
                    pe.wait_ge(n_act, 4 * g - 8 + 2)
                pe.wait_ge(c_dve, 5 * g + 5)

            def project_out(b, pairs):
                settled(pairs)
                pe.wait_ge(on_ready, b + 1)
                for t in range(TILES):
                    last = nc.tensor.matmul(bank[t // 4][:, t % 4 * 128:(t % 4 + 1) * 128],
                                            ONN[:, t * 128:(t + 1) * 128], w["o1"], start=True, stop=True)
                    if t % 4 == 3:
                        last.then_inc(y_ready, 1)
                pe.wait_ge(y_taken, 2 * b + 2)

            def project_gates(b, pairs):
                settled(pairs)
                pe.wait_ge(on_ready, B + b + 1)
                for t in range(TILES):
                    last = nc.tensor.matmul(bank[t // 3][:, t % 3 * OUTW:(t % 3 + 1) * OUTW],
                                            ONN[:, t * 128:(t + 1) * 128], w["p2"], start=True, stop=True)
                    if t % 3 == 2 or t == TILES - 1:
                        last.then_inc(z_ready, 1)
                pe.wait_ge(z_taken, 3 * b + 3)

            pe.wait_ge(w_loaded, 48)
            project(0, 1, 0)
            for qt in range(TILES):
                maxima(0, 0, qt, 64 if qt == 0 else None)
            turn_maxima(0, 0)
            for qt in range(AHEAD):
                maxima(1, 1, qt, 64 if qt == 0 else None)
            body(0, first=True)
            body(1)
            project(1, 1, 4)
            for b in range(B):
                with pe.Fori(4 * b + 2, 4 * b + 5) as it:
                    body(it)
                project_out(b, 8 * b + 10)
                body(4 * b + 5)
                project(b + 2, 2, 8 * b + 12)
            with pe.Fori(10, 13) as it:
                body(it)
            project_gates(0, 26)
            with pe.Fori(13, 15) as it:
                body(it)
            body(15, last=True)
            values(ALL_PAIRS - 1, 1, TILES - 1)
            pe.wait_ge(exp_done, 4 * TILES * ALL_PAIRS)
            pe.wait_ge(on_ready, 2 * B)
            for t in range(TILES):
                last = nc.tensor.matmul(bank[t // 3][:, t % 3 * OUTW:(t % 3 + 1) * OUTW],
                                        ONN[:, t * 128:(t + 1) * 128], w["p2"], start=True, stop=True)
                if t % 3 == 2 or t == TILES - 1:
                    last.then_inc(z_ready, 1)

        @block.scalar
        def _(act):
            def pair(p, u, it, first=False):
                for s in range(TILES):
                    step = TILES * p + s
                    for j in range(4):
                        n = 4 * step + j
                        act.wait_ge(st_ready, n + 1)
                        if j == 0:
                            wait(act, pv_done, step - 1)
                        nc.scalar.activation(PT[:, s % 2, j, :], ST[:, j % 2, :], ACT.Exp).then_inc(exp_done, 1)
                    if s == 1 and not first:
                        copy_out(p, 1 - u, 64 * (it - 1 + u))

            def copy_out(pairs, u, stored):
                act.wait_ge(pv_done, TILES * pairs)
                wait(act, e_store[u], stored)
                nc.scalar.copy(E[:, u, :], PV[:, :]).then_inc(evac, 1)

            def body(it, first=False):
                pair(2 * it, 0, it, first)
                pair(2 * it + 1, 1, it)

            def norm(g):
                act.wait_ge(var_ready, g + 1)
                nc.scalar.activation(lnv[:, :], var[:, :], ACT.Ln).then_inc(rs_act, 1)
                act.wait_ge(rs_act, 2 * g + 1)
                nc.scalar.activation(rs0[:, :], lnv[:, :], ACT.Exp, scale=-0.5).then_inc(rs_act, 1)

            def project(g, layer):
                act.wait_ge(c_ready, 8 * g + 1)
                nc.scalar.copy(XNT[:, 0:HALF], bank[0]).then_inc(c_act, 1)
                bias = qbias[:, :] if layer == 1 else col["bq2"]
                scale = DH ** -0.5 if layer == 1 else 1.0
                act.wait_ge(c_ready, 8 * g + 3)
                wait(act, parts_stored, 2 * COMBOS * 16 * g)
                nc.scalar.activation(QT[:, 0:HALF], bank[2], ACT.Identity, bias=bias, scale=scale).then_inc(c_act, 1)
                act.wait_ge(c_ready, 8 * g + 4)
                nc.scalar.activation(QT[:, HALF:S], bank[0], ACT.Identity, bias=bias, scale=scale).then_inc(c_act, 1)
                if layer == 2:
                    r = g - 2
                    for n in range(2):
                        act.wait_ge(n_ready, 2 * r + n + 1)
                        nc.scalar.copy(N2[:, n * HALF:(n + 1) * HALF], bank[2 - 2 * n]).then_inc(n_act, 1)
                    act.wait_ge(n_act, 4 * r + 2)
                    nc.scalar.activation(LN2[:, :], N2[:, :], ACT.Ln).then_inc(n_act, 1)
                    act.wait_ge(n_act, 4 * r + 3)
                    nc.scalar.activation(Y[:, :], LN2[:, :], ACT.Exp, scale=-0.5).then_inc(n_act, 1)

            def gates(b):
                act.wait_ge(g_dve, G_STEPS * b + G_BEFORE)
                nc.scalar.activation(GE[:, :, :], GL[:, :, :], ACT.Exp).then_inc(g_act, 1)

            act.wait_ge(small_ready, 3)
            nc.scalar.activation(soft[:, 1:2], soft[:, 0:1], ACT.Exp, scale=-1.0).then_inc(small_act, 1)
            act.wait_ge(small_act, 1)
            nc.scalar.activation(soft[:, 2:3], soft[:, 1:2], ACT.Ln, bias=1.0).then_inc(small_act, 1)
            norm(0)
            project(0, 1)
            norm(1)
            body(0, first=True)
            body(1)
            project(1, 1)
            for b in range(B):
                with act.Fori(4 * b + 2, 4 * b + 5) as it:
                    body(it)
                norm(b + 2)
                body(4 * b + 5)
                project(b + 2, 2)
            with act.Fori(10, 13) as it:
                body(it)
            gates(0)
            with act.Fori(13, 16) as it:
                body(it)
            copy_out(ALL_PAIRS, 1, 64 * (ALL_PAIRS // 2 - 1))
            gates(1)

        @block.vector
        def _(dve):
            def maximum(pm, u, qt):
                for hh in range(2):
                    dve.wait_ge(mx_ready, 2 * TILES * pm + 2 * qt + hh + 1)
                    c = hh * TILES + qt
                    nc.vector.tensor_reduce(NM[:, u, c:c + 1], MX[:, hh, :], AX.X, ALU.max, negate=True)\
                      .then_inc(mx_taken, 1)

            def split_maxima(pm, u, stored):
                dve.wait_ge(mt_ready, pm + 1)
                wait(dve, ld_m[u], stored)
                nc.vector.tensor_copy(NB[:, u, 0, :], XB[0:2 * TILES, 0:128]).then_inc(nm_first, 1)
                dve.wait_ge(nm_first, pm + 1)
                nc.vector.tensor_tensor(NB[:, u, 1, :], XB[0:2 * TILES, 0:128], NB[:, u, 0, :], ALU.subtract)\
                  .then_inc(nm_ready, 1)

            def pair(p, u, it, left=2):
                for s in range(TILES):
                    if s < TILES - AHEAD:
                        if left >= 1:
                            maximum(p + 1, 1 - u, s + AHEAD)
                    elif left >= 2:
                        maximum(p + 2, u, s - (TILES - AHEAD))
                    if s == TILES - 2 and left >= 1:
                        split_maxima(p + 1, 1 - u, 64 * (it + u))

            def body(it, last=False):
                pair(2 * it, 0, it, left=1 if last else 2)
                pair(2 * it + 1, 1, it, left=0 if last else 2)

            def norm(g, b):
                steps = [0]

                def then(ins):
                    steps[0] += 1
                    ins.then_inc(ln_dve, 1)

                def ready():
                    dve.wait_ge(ln_dve, 6 * g + steps[0])

                Xb = X[:, b] if isinstance(b, int) else X[:, bass.ds(b, 1)].rearrange("p o t c -> p (o t) c")
                for t in range(TILES):
                    last = nc.vector.bn_stats(stats[:, t, :], Xb[:, t, :])
                then(last)
                ready()
                for t in range(TILES):
                    last = nc.vector.bn_aggr(mv[:, t, :], stats[:, t, :])
                then(last)
                ready()
                nc.vector.tensor_scalar(var[:, :], mv[:, :, 1], EPS, None, ALU.add).then_inc(var_ready, 1)
                dve.wait_ge(rs_act, 2 * g + 2)
                dve.wait_ge(var_ready, g + 1)
                then(nc.vector.tensor_tensor(rst[:, :], rs0[:, :], rs0[:, :], ALU.mult))
                ready()
                then(nc.vector.tensor_tensor(rst[:, :], rst[:, :], var[:, :], ALU.mult))
                ready()
                then(nc.vector.tensor_scalar(rst[:, :], rst[:, :], -0.5, 1.5, ALU.mult, ALU.add))
                ready()
                then(nc.vector.tensor_tensor(rstd[:, :], rs0[:, :], rst[:, :], ALU.mult))
                ready()
                wait(dve, c_ready, 8 * g)
                for t in range(TILES):
                    last = nc.vector.tensor_scalar(XN[:, t, :], Xb[:, t, :], mv[:, t, 0:1], rstd[:, t:t + 1],
                                                   ALU.subtract, ALU.mult)
                last.then_inc(xn_ready, 1)
                assert steps[0] == 6

            def project(g, layer):
                dve.wait_ge(c_ready, 8 * g + 2)
                nc.vector.tensor_copy(XNT[:, HALF:S], bank[1]).then_inc(c_dve, 1)
                for n in range(2):
                    dve.wait_ge(c_ready, 8 * g + 5 + n)
                    if n == 0:
                        wait(dve, parts_stored, 2 * COMBOS * 16 * g)
                    nc.vector.tensor_scalar(KT[:, n * HALF:(n + 1) * HALF], bank[1 + n], col[f"bk{layer}"],
                                            None, ALU.add).then_inc(c_dve, 1)
                for n in range(2):
                    dve.wait_ge(c_ready, 8 * g + 7 + n)
                    for t in range(4):
                        k = 4 * n + t
                        where = VA[:, bass.ds(PAIRS * g, PAIRS), :]\
                            .rearrange("p j (e k d) -> p j e k d", e=2, k=TILES)[:, :, :, k, 0:DH]\
                            .rearrange("p j e d -> p (j e) d")
                        last = nc.vector.tensor_tensor(
                            where, bank[n][:, t * 128:(t + 1) * 128].rearrange("p (h d) -> p h d", d=DH),
                            row[f"bv{layer}"].rearrange("p (h d) -> p h d", d=DH), ALU.add)
                    last.then_inc(c_dve, 1)

            def divide(e):
                dve.wait_ge(on_loaded, 64 * e + 64)
                nc.vector.reciprocal(RDEN[:, :], DEN[:, :]).then_inc(e_dve, 1)
                dve.wait_ge(e_dve, e + 1)
                nc.vector.tensor_tensor(ONN[:, :], ON[:, :], RDEN[:, :], ALU.mult).then_inc(on_ready, 1)

            def residual(b):
                dve.wait_ge(biased, b + 1)
                for n in range(2):
                    dve.wait_ge(y_ready, 2 * b + n + 1)
                    Xh = X[:, bass.ds(b, 1), 4 * n:4 * n + 4, :].rearrange("p o t c -> p (o t c)")
                    nc.vector.tensor_tensor(Xh, bank[n], Xh, ALU.add).then_inc(y_taken, 1)
                dve.wait_ge(y_taken, 2 * b + 2)

            def gates(b):
                steps = [0]

                def then(ins):
                    steps[0] += 1
                    ins.then_inc(g_dve, 1)
                    dve.wait_ge(g_dve, G_STEPS * b + steps[0])

                for n in range(3):
                    dve.wait_ge(z_ready, 3 * b + n + 1)
                    m = min(3, TILES - 3 * n)
                    nc.vector.tensor_copy(Z[:, 3 * n:3 * n + m, :],
                                          bank[n][:, 0:m * OUTW].rearrange("p (t c) -> p t c", t=m))\
                      .then_inc(z_taken, 1)
                dve.wait_ge(z_taken, 3 * b + 3)
                then(nc.vector.tensor_tensor(GL[:, :, :], Z[:, :, D:OUTW],
                                             row["brs"].unsqueeze(1).to_broadcast([128, TILES, NG + 2]), ALU.add))
                part = [slice(0, NG), slice(NG, NG + 2)]
                for i in range(2):
                    then(nc.vector.tensor_reduce(GM[:, i, :], GL[:, :, part[i]], AX.X, ALU.max))
                for i in range(2):
                    n = part[i].stop - part[i].start
                    then(nc.vector.tensor_tensor(GL[:, :, part[i]], GL[:, :, part[i]],
                                                 GM[:, i, :].unsqueeze(2).to_broadcast([128, TILES, n]),
                                                 ALU.subtract))
                assert steps[0] == G_BEFORE
                dve.wait_ge(g_act, b + 1)
                for t in range(TILES):
                    last = nc.vector.max(T8[:, t, :], GE[:, t, 0:NG])
                then(last)
                for i in range(2):
                    then(nc.vector.tensor_reduce(GS[:, i, :], GE[:, :, part[i]], AX.X, ALU.add))
                then(nc.vector.reciprocal(GR[:, :, :], GS[:, :, :]))
                then(nc.vector.tensor_reduce(G3[:, 0, :], T8[:, :, 0:TOP], AX.X, ALU.add))
                then(nc.vector.tensor_tensor(G3[:, 0, :], G3[:, 0, :], GR[:, 0, :], ALU.mult))
                then(nc.vector.tensor_tensor(SW[:, :, :], GE[:, :, part[1]],
                                             GR[:, 1, :].unsqueeze(2).to_broadcast([128, TILES, 2]), ALU.mult))
                then(nc.vector.tensor_tensor(G3[:, 1, :], SW[:, :, 0], SW[:, :, 1], ALU.add))
                then(nc.vector.tensor_tensor(G3[:, 1, :], G3[:, 1, :], SW[:, :, 0], ALU.mult))
                then(nc.vector.tensor_tensor(G3[:, 2, :], G3[:, 0, :], SW[:, :, 1], ALU.mult))
                then(nc.vector.tensor_scalar(G3[:, 1, :], G3[:, 1, :], 2.0, None, ALU.mult))
                then(nc.vector.tensor_scalar(G3[:, 2, :], G3[:, 2, :], 2.0 * TOP, None, ALU.mult))
                then(nc.vector.tensor_tensor(gate[:, :], G3[:, 1, :], G3[:, 2, :], ALU.add))
                dve.wait_ge(biased, B + b + 1)
                for t in range(TILES):
                    last = nc.vector.scalar_tensor_tensor(X[:, b, t, :], Z[:, t, 0:D], gate[:, t:t + 1],
                                                          X[:, b, t, :], ALU.mult, ALU.add)
                last.then_inc(out_ready, 1)
                assert steps[0] == G_STEPS, steps[0]

            nc.vector.memset(STK[:, :, :], 1.0).then_inc(fill_ready, 1)
            for tile in (MXQ, MXK, STQ):
                nc.vector.memset(tile[:].bitcast(F32), 0.0).then_inc(fill_ready, 1)
            nc.vector.memset(PV[:, :], 0.0).then_inc(small_ready, 1)
            dve.wait_ge(w_loaded, 48)
            nc.vector.tensor_scalar(qbias[:, :], col["bq1"], DH ** -0.5, None, ALU.mult).then_inc(small_ready, 1)
            nc.vector.scalar_tensor_tensor(soft[:, 0:1], col["temp"], -1.0, col["temp"], ALU.mult, ALU.max)\
              .then_inc(small_ready, 1)
            dve.wait_ge(x_loaded[0], 16)
            norm(0, 0)
            dve.wait_ge(small_act, 2)
            nc.vector.scalar_tensor_tensor(head_scale[:, :], col["temp"], 0.0, soft[:, 2:3], ALU.max, ALU.add)\
              .then_inc(small_ready, 1)
            dve.wait_ge(small_ready, 4)
            nc.vector.tensor_scalar(head_scale[:, :], head_scale[:, :], DH ** -0.5, None, ALU.mult)\
              .then_inc(small_ready, 1)
            dve.wait_ge(ones_ready, 1)
            project(0, 1)
            for qt in range(TILES):
                maximum(0, 0, qt)
            split_maxima(0, 0, 0)
            for qt in range(AHEAD):
                maximum(1, 1, qt)
            dve.wait_ge(x_loaded[1], 16)
            norm(1, 1)
            body(0)
            body(1)
            project(1, 1)
            for b in range(B):
                with dve.Fori(4 * b + 2, 4 * b + 5) as it:
                    body(it)
                divide(b)
                residual(b)
                norm(b + 2, b)
                body(4 * b + 5)
                project(b + 2, 2)
            with dve.Fori(10, 13) as it:
                body(it)
            divide(2)
            gates(0)
            with dve.Fori(13, 15) as it:
                body(it)
            body(15, last=True)
            divide(3)
            gates(1)

        @block.gpsimd
        def _(pool):
            nc.gpsimd.memset(VA[:, :, :], 1.0).then_inc(ones_ready, 1)
            pool.wait_ge(w_loaded, 48)

            def split(src, parts, s, done):
                k = [0]

                def then(ins):
                    k[0] += 1
                    ins.then_inc(s, 1)
                    pool.wait_ge(s, done + k[0])

                then(nc.gpsimd.tensor_copy(parts[:, 0, :], src[:, :]))
                then(nc.gpsimd.tensor_tensor(QR[:, :], src[:, :], parts[:, 0, :], ALU.subtract))
                then(nc.gpsimd.tensor_copy(parts[:, 1, :], QR[:, :]))
                then(nc.gpsimd.tensor_tensor(parts[:, 2, :], QR[:, :], parts[:, 1, :], ALU.subtract))

            def store(scratch, parts, order, g):
                rows = scratch[bass.ds(H * g, H)]
                for c, part in enumerate(order):
                    pool.dma_start(rows[:, c * DH:(c + 1) * DH, :], parts[:, part, :]).then_inc(parts_stored, 16)

            def project1(g):
                pool.wait_ge(c_act, 3 * g + 3)
                split(QT, QB, pool1, 8 * g)
                store(qc, QB, Q_PART, g)
                pool.wait_ge(c_dve, 5 * g + 3)
                split(KT, KB, pool1, 8 * g + 4)
                store(kc, KB, K_PART, g)

            def project2(g):
                r = g - 2
                n = 14 * r
                pool.wait_ge(c_act, 3 * g + 3)
                nc.gpsimd.tensor_tensor(SQ[:, :], QT[:, :], QT[:, :], ALU.mult).then_inc(sq_ready, 1)
                pool.wait_ge(c_dve, 5 * g + 3)
                split(KT, KB, pool2, n)
                store(kc, KB, K_PART, g)
                pool.wait_ge(n_act, 4 * r + 4)
                k = [n + 4]

                def then(ins):
                    k[0] += 1
                    ins.then_inc(pool2, 1)
                    pool.wait_ge(pool2, k[0])

                then(nc.gpsimd.tensor_tensor(SQ[:, :], Y[:, :], Y[:, :], ALU.mult))
                then(nc.gpsimd.tensor_tensor(SQ[:, :], SQ[:, :], N2[:, :], ALU.mult))
                then(nc.gpsimd.tensor_scalar(SQ[:, :], SQ[:, :], -0.5, 1.5, ALU.mult, ALU.add))
                then(nc.gpsimd.tensor_tensor(Y[:, :], Y[:, :], SQ[:, :], ALU.mult))
                then(nc.gpsimd.tensor_tensor(QT[:, :], QT[:, :], Y[:, :], ALU.mult))
                then(nc.gpsimd.tensor_scalar(QT[:, :], QT[:, :], col["qe"], head_scale[:, :], ALU.add, ALU.mult))
                split(QT, QB, pool2, k[0])
                store(qc, QB, Q_PART, g)

            def reload(e, b, bias):
                for u in range(2):
                    pool.wait_ge(e_store[u], 256 * e + 256)
                wait(pool, on_ready, e)
                for qh in range(2):
                    here = slice(qh * HALF, (qh + 1) * HALF)
                    src = os_[bass.ds(H * e, H), qh]
                    pool.dma_start(ON[:, here], src[:, 0:DH, :]).then_inc(on_loaded, 16)
                    pool.dma_start(DEN[:, here], src[:, DH:VROW, :].to_broadcast([H, DH, HALF]))\
                        .then_inc(on_loaded, 16)
                Xb = X[:, bass.ds(b, 1)].rearrange("p o t c -> p (o t) c")
                nc.gpsimd.tensor_tensor(Xb, Xb, row[bias].unsqueeze(1).to_broadcast([128, TILES, D]), ALU.add)\
                  .then_inc(biased, 1)

            project1(0)
            project1(1)
            for b in range(B):
                pool.wait_ge(xn_ready, b + 1)
                reload(b, b, "bo1")
                project2(b + 2)
            for b in range(B):
                pool.wait_ge(xn_ready, B + b + 1)
                reload(B + b, b, "bp")


_INS = ["x", "wmat", "wcol", "wrow"]


def kernel(**inputs):
    import numpy as np
    import concourse.bacc as bacc
    from concourse.bass_utils import run_bass_kernel_spmd

    a = {n: np.asarray(v) for n, v in inputs.items()}
    L1 = {n: a["L0_attn_" + n] for n in ("x", "Wq", "bq", "Wk", "bk", "Wv", "bv", "Wo", "bo")}
    L2 = {n: a["L0_ffn_" + n] for n in ("Wq", "bq", "Wk", "bk", "Wv", "bv", "Wp", "bp", "Wr", "br", "Ws", "bs",
                                         "temperature", "query_embedding")}
    f = np.float32
    eye = np.eye(D, dtype=f)
    heads = np.kron(np.eye(H, dtype=f), np.ones((DH, DH), f))
    arrays = {
        "x": np.ascontiguousarray(L1["x"].reshape(B * S, D)),
        "wmat": np.ascontiguousarray(np.concatenate(
            [L1["Wq"].T, L1["Wk"].T, L1["Wv"].T, L1["Wo"].T, L2["Wq"].T, L2["Wk"].T, L2["Wv"].T,
             L2["Wp"].T, L2["Wr"].T, L2["Ws"].T, eye, heads], axis=1)),
        "wcol": np.ascontiguousarray(np.stack(
            [L1["bq"], L1["bk"], L2["bq"], L2["bk"], L2["query_embedding"].reshape(D),
             np.repeat(L2["temperature"].reshape(H), DH)], axis=1)),
        "wrow": np.ascontiguousarray(np.concatenate(
            [L1["bv"], L1["bo"], L2["bv"], L2["bp"], L2["br"], L2["bs"]]).reshape(1, R_WIDTH)),
    }
    nc = bacc.Bacc("TRN2", target_bir_lowering=False, num_devices=1)
    args = [nc.dram_tensor(n, arrays[n].shape, F32, kind="ExternalInput").ap() for n in _INS]
    args.append(nc.dram_tensor("out", (B * S, D), F32, kind="ExternalOutput").ap())
    args.append(nc.dram_tensor("q_parts", (SEGMENTS * H, CROWS, S), BF16).ap())
    args.append(nc.dram_tensor("k_parts", (SEGMENTS * H, CROWS, S), BF16).ap())
    args.append(nc.dram_tensor("head_sums", (SEGMENTS * H, 2, VROW, HALF), F32).ap())
    moe_attention_program(nc, *args)
    r = run_bass_kernel_spmd(nc, [arrays], core_ids=[0])
    return np.asarray(r.results[0]["out"]).reshape(B, S, D)
```

```python
import concourse.bass as bass
from concourse import mybir
from contextlib import ExitStack

F32 = mybir.dt.float32
BF16 = mybir.dt.bfloat16
ALU = mybir.AluOpType
ACT = mybir.ActivationFunctionType
AX = mybir.AxisListType

B, S, D, H = 2, 1024, 128, 16
DH = D // H
TILES = S // 128
HALF = 512
PAIRS = H // 2
SEGMENTS = 2 * B
ALL_PAIRS = SEGMENTS * PAIRS
NG = H - 1
TOP = 3
EPS = 1e-5

COMBOS = 6
CROWS = COMBOS * DH
SROWS = CROWS + 2
MROWS = 3 * DH
VROW = DH + 1
VPAIR = 2 * TILES * VROW
AHEAD = 4

W_COLS = {}
_at = 0
for _name, _n in (("q1", D), ("k1", D), ("v1", D), ("o1", D), ("q2", D), ("k2", D), ("v2", D),
                  ("p2", D + NG + 2), ("ident", D), ("same_head", D)):
    W_COLS[_name] = (_at, _at + _n)
    _at += _n
W_WIDTH = _at
COLS = ["bq1", "bk1", "bq2", "bk2", "qe", "temp"]
R_COLS = {}
_at = 0
for _name, _n in (("bv1", D), ("bo1", D), ("bv2", D), ("bp", D), ("brs", NG + 2)):
    R_COLS[_name] = (_at, _at + _n)
    _at += _n
R_WIDTH = _at
OUTW = D + NG + 2


EXTRA = {}


def _plan():
    def put(at, kind, g, n):
        EXTRA[at] = (kind, g, n)

    for at, kind, n in (((1, 0), "t", 0), ((1, 1), "t", 1), ((1, 2), "q", 0), ((1, 3), "q", 1),
                        ((1, 6), "k", 0), ((1, 7), "k", 1), ((2, 0), "v", 0), ((2, 1), "v", 1)):
        put(at, kind, 1, n)
    for b in range(B):
        p = PAIRS * (b + 1) + 1
        for s, kind, n in ((1, "y", 0), (2, "y", 1), (8, "t", 0), (9, "t", 1), (10, "q", 0), (11, "q", 1),
                           (14, "n", 0), (15, "n", 1), (16, "k", 0), (17, "k", 1), (18, "v", 0), (19, "v", 1)):
            put((p + s // TILES, s % TILES), kind, b if kind == "y" else B + b, n)
    for n in range(3):
        put((ALL_PAIRS - 1, n + 1), "z", 0, n)


_plan()
SUMS_STEP, SUMS_AT = 3, [PAIRS, 2 * PAIRS, ALL_PAIRS - 2]
TURN_STEP = 5


def extra_at(p, s):
    return [EXTRA[p, s]] if isinstance(p, int) and (p, s) in EXTRA else []


def extras_before(p, s=0):
    return sum(at < (p, s) for at in EXTRA)


def moe_attention_program(nc, x, wmat, wcol, wrow, out, qc, kc, os_, rs_):
    ctx = ExitStack()
    with ctx:
        def sb(name, shape, dt=F32):
            return ctx.enter_context(nc.sbuf_tensor(name, shape, dt))

        def sem(name):
            return ctx.enter_context(nc.semaphore(name))

        X = sb("X", [128, B, TILES, D])
        W = sb("W", [128, W_WIDTH])
        C = sb("C", [128, len(COLS)])
        R = sb("R", [128, R_WIDTH])
        col = {n: C[:, i:i + 1] for i, n in enumerate(COLS)}
        w = {n: W[:, a:b] for n, (a, b) in W_COLS.items()}
        row = {n: R[:, a:b] for n, (a, b) in R_COLS.items()}
        qbias = sb("qbias", [128, 1])
        head_scale = sb("head_scale", [128, 1])
        soft = sb("soft", [128, 3])
        stats = sb("stats", [128, TILES, 6])
        mv = sb("mv", [128, TILES, 2])
        var = sb("var", [128, TILES])
        half_neg = sb("half_neg", [128, TILES])
        rstd = sb("rstd", [128, TILES])
        shift = sb("shift", [128, TILES])
        XN = sb("XN", [128, TILES, D])
        XNT = sb("XNT", [128, S])
        QT = sb("QT", [128, S])
        QR = sb("QR", [128, S])
        KR = sb("KR", [128, S])
        QB = sb("QB", [128, 3, S], BF16)
        KB = sb("KB", [128, 3, S], BF16)
        SQ = sb("SQ", [128, S])
        N2 = sb("N2", [128, S])
        LN2 = sb("LN2", [128, S])
        Y = sb("Y", [128, S])
        VA = sb("VA", [128, ALL_PAIRS, VPAIR])
        STQ = sb("STQ", [128, 2, 2, S], BF16)
        STK = sb("STK", [128, 2, S], BF16)
        MXQ = sb("MXQ", [128, 2, 2, S], BF16)
        MXK = sb("MXK", [128, 2, S], BF16)
        VR = sb("VR", [128, 2, VPAIR])
        NM = sb("NM", [128, 2, 2 * TILES])
        NB = sb("NB", [2 * TILES, 2, 2, 128], BF16)
        PT = sb("PT", [128, 2, 4, HALF])
        E = sb("E", [128, 2, HALF])
        ON = sb("ON", [128, S])
        DEN = sb("DEN", [128, S])
        DC = sb("DC", [128, 128])
        RC = sb("RC", [128, 128])
        RDEN = sb("RDEN", [128, S])
        ONN = sb("ONN", [128, S])
        Z = sb("Z", [128, TILES, OUTW])
        GL = sb("GL", [128, TILES, NG + 2])
        GE = sb("GE", [128, TILES, NG + 2])
        GM = sb("GM", [128, 2, TILES])
        T8 = sb("T8", [128, TILES, 8])
        GS = sb("GS", [128, 2, TILES])
        GR = sb("GR", [128, 2, TILES])
        G3 = sb("G3", [128, 3, TILES])
        SW = sb("SW", [128, TILES, 2])
        gate = sb("gate", [128, TILES])

        ST = ctx.enter_context(nc.psum_tensor("ST", [128, 2, HALF], F32))
        MX = ctx.enter_context(nc.psum_tensor("MX", [128, 2, 2 * HALF], F32))
        PV = ctx.enter_context(nc.psum_tensor("PV", [128, HALF], F32))
        XB = ctx.enter_context(nc.psum_tensor("XB", [128, HALF], F32))
        last_bank = [ST[:, 0, :], ST[:, 1, :], XB[:, :]]
        first_bank = {("t", 0): ST[:, 0, :], ("t", 1): ST[:, 1, :], ("q", 0): MX[:, 0, 0:HALF],
                      ("q", 1): MX[:, 0, HALF:], ("k", 0): MX[:, 1, 0:HALF], ("k", 1): MX[:, 1, HALF:],
                      ("v", 0): XB[:, :], ("v", 1): PV[:, :]}
        FIRST = [("t", 0), ("t", 1), ("q", 0), ("k", 0), ("q", 1), ("k", 1), ("v", 0), ("v", 1)]

        x_loaded = [sem(f"x_loaded{b}") for b in range(B)]
        w_loaded = sem("w_loaded")
        ones_ready = sem("ones_ready")
        fill_ready = sem("fill_ready")
        scaled = sem("scaled")
        pv_zero = sem("pv_zero")
        small_act = sem("small_act")
        small_ready = sem("small_ready")
        ld_mx = [sem(f"ld_mx{u}") for u in range(2)]
        ld_st = [sem(f"ld_st{u}") for u in range(2)]
        ld_m = [sem(f"ld_m{u}") for u in range(2)]
        st_ready, exp_done = sem("st_ready"), sem("exp_done")
        mx_ready, mx_taken = sem("mx_ready"), sem("mx_taken")
        mt_ready, nm_first, nm_ready = sem("mt_ready"), sem("nm_first"), sem("nm_ready")
        pv_done, evac = sem("pv_done"), sem("evac")
        e_store = [sem(f"e_store{u}") for u in range(2)]
        first_full = sem("first_full")
        xb_full = sem("xb_full")
        stats_dve, var_ready, ln_pool, xn_ready = sem("stats_dve"), sem("var_ready"), sem("ln_pool"), sem("xn_ready")
        xnt_ready = sem("xnt_ready")
        q_first, q_rest, q_second = sem("q_first"), sem("q_rest"), sem("q_second")
        k_first, k_rest, k_second = sem("k_first"), sem("k_rest"), sem("k_second")
        v_ready, sq_act, n_act = sem("v_ready"), sem("sq_act"), sem("n_act")
        q_third, k_third, q_pool = sem("q_third"), sem("k_third"), sem("q_pool")
        first_main, first_rest = sem("first_main"), sem("first_rest")
        main_stored, rest_stored = sem("main_stored"), sem("rest_stored")
        on_loaded, dc_loaded, dc_ready, rc_stored, r_loaded = (sem("on_loaded"), sem("dc_loaded"),
                                                               sem("dc_ready"), sem("rc_stored"), sem("r_loaded"))
        on_ready, last_dve = sem("on_ready"), sem("last_dve")
        biased, y_taken = sem("biased"), sem("y_taken")
        z_ready, z_taken = sem("z_ready"), sem("z_taken")
        g_dve, g_act, out_ready, out_stored = sem("g_dve"), sem("g_act"), sem("out_ready"), sem("out_stored")

        ITERATIONS = ALL_PAIRS // 2
        SPANS = [(0, 1), (1, 2), (2, 4), (4, 5), (5, 6), (6, 8), (8, 9), (9, 10), (10, 15), (15, 16)]

        def xb_use(p, s):
            return p + 1 + extras_before(p, s) + (s >= TURN_STEP)

        G_STEPS, G_BEFORE = 18, 5
        block = ctx.enter_context(nc.Block())

        def wait(eng, s, value):
            if not isinstance(value, int) or value > 0:
                eng.wait_ge(s, value)

        def store_main(eng, g, q=True):
            scratch, B3, slots = (qc, QB, (0, 0, 1)) if q else (kc, KB, (1, 2, 2))
            for c, slot in enumerate(slots):
                eng.dma_start(scratch[c, D * g:D * (g + 1), :], B3[:, slot, :])\
                   .then_inc(main_stored if g else first_main, 16)

        def store_rest(eng, g, q=True):
            scratch, B3 = (qc, QB) if q else (kc, KB)
            eng.dma_start(scratch[3:6, D * g:D * (g + 1), :].rearrange("c p t -> p c t"), B3[:, :, :])\
               .then_inc(rest_stored if g else first_rest, 16)

        MAIN, REST = 6 * 16, 2 * 16

        @block.sync
        def _(sp):
            for b in range(B):
                sp.dma_start(X[:, b], x[b * S:(b + 1) * S].rearrange("(t p) c -> p t c", p=128))\
                  .then_inc(x_loaded[b], 16)
                if b == 0:
                    sp.dma_start(W[:, :], wmat).then_inc(w_loaded, 16)
                    sp.dma_start(C[:, :], wcol).then_inc(w_loaded, 16)
                    sp.dma_start(R[:, :], wrow.to_broadcast([128, R_WIDTH])).then_inc(w_loaded, 16)

            def load_max(p, u):
                for hh in range(2):
                    rows = slice(64 * hh, 64 * hh + MROWS)
                    sp.dma_start(MXQ[rows, u, hh, :], qc[0:3, bass.ds(DH * (2 * p + hh), DH), :]).then_inc(ld_mx[u], 16)
                    sp.dma_start(MXK[rows, u, :], kc[0:3, bass.ds(DH * (2 * p + hh), DH), :]).then_inc(ld_mx[u], 16)

            def load_scores(p, u):
                for hh in range(2):
                    sp.dma_start(STQ[64 * hh:64 * hh + CROWS, u, hh, :], qc[:, bass.ds(DH * (2 * p + hh), DH), :])\
                      .then_inc(ld_st[u], 16)
                    sp.dma_start(STK[64 * hh:64 * hh + CROWS, u, :], kc[:, bass.ds(DH * (2 * p + hh), DH), :])\
                      .then_inc(ld_st[u], 16)
                sp.dma_start(VR[:, u, :], VA[:, bass.ds(p, 1), :]).then_inc(ld_st[u], 16)

            def load_shift(u):
                for hh in range(2):
                    for part in range(2):
                        r = 64 * hh + CROWS + part
                        sp.dma_start(STQ[r:r + 1, u, hh, :], NB[TILES * hh:TILES * (hh + 1), u, part, :])\
                          .then_inc(ld_m[u], 16)

            def store_result(p, u):
                for hh in range(2):
                    for qh in range(2):
                        g = 2 * hh + qh
                        sp.dma_start(os_[bass.ds(2 * p + hh, 1), qh], E[32 * g:32 * g + VROW, u, :])\
                          .then_inc(e_store[u], 16)

            def pair(p, u, first=False, left=3):
                if left >= 1:
                    if not first:
                        sp.wait_ge(pv_done, TILES * p)
                    load_scores(p + 1, 1 - u)
                if not first:
                    sp.wait_ge(evac, p)
                    store_result(p - 1, 1 - u)
                if left >= 3:
                    sp.wait_ge(mx_ready, 2 * TILES * (p + 2))
                    load_max(p + 3, 1 - u)
                if left >= 1:
                    sp.wait_ge(nm_ready, p + 2)
                    load_shift(1 - u)

            sp.wait_ge(fill_ready, 4)
            sp.wait_ge(q_second, 2)
            store_main(sp, 0)
            sp.wait_ge(k_second, 2)
            store_main(sp, 0, q=False)
            sp.wait_ge(first_main, MAIN)
            load_max(0, 0)
            load_max(1, 1)
            sp.wait_ge(q_third, 1)
            store_rest(sp, 0)
            sp.wait_ge(k_third, 1)
            store_rest(sp, 0, q=False)
            sp.wait_ge(first_rest, REST)
            sp.wait_ge(v_ready, 2)
            load_scores(0, 0)
            sp.wait_ge(nm_ready, 1)
            load_shift(0)
            sp.wait_ge(mx_ready, 2 * TILES)
            load_max(2, 0)
            pair(0, 0, first=True)
            with sp.Fori(0, 2) as k:
                pair(2 * k + 1, 1)
                pair(2 * k + 2, 0)
            for g in range(SEGMENTS - 1):
                sp.wait_ge(main_stored, MAIN * (g + 1))
                sp.wait_ge(rest_stored, REST * (g + 1))
                sp.wait_ge(v_ready, 2 * (g + 2))
                with sp.Fori(4 * g + 2, 4 * g + 6) as k:
                    pair(2 * k + 1, 1)
                    pair(2 * k + 2, 0)
            for left in (2, 1, 0):
                p = ALL_PAIRS - 1 - left
                pair(p, p % 2, left=left)
            sp.wait_ge(evac, ALL_PAIRS)
            store_result(ALL_PAIRS - 1, 1)
            for b in range(B):
                sp.wait_ge(out_ready, b + 1)
                sp.dma_start(out[b * S:(b + 1) * S].rearrange("(t p) c -> p t c", p=128), X[:, b])\
                  .then_inc(out_stored, 16)
            sp.wait_ge(out_stored, 16 * B)
            sp.wait_ge(rc_stored, 16 * 3)
            for u in range(2):
                sp.wait_ge(e_store[u], ALL_PAIRS // 2 * 64)

        @block.tensor
        def _(pe):
            def maxima(pm, u, qt, loaded=None):
                if loaded is not None:
                    pe.wait_ge(ld_mx[u], loaded)
                for hh in range(2):
                    wait(pe, mx_taken, 2 * TILES * pm + 2 * qt + hh - 1)
                    for kh in range(2):
                        here = slice(kh * HALF, (kh + 1) * HALF)
                        last = nc.tensor.matmul(MX[:, hh, here], MXQ[:, u, hh, qt * 128:(qt + 1) * 128],
                                                MXK[:, u, here], start=True, stop=True)
                    last.then_inc(mx_ready, 1)

            bank_use = [None]

            def wait_bank(turned):
                if bank_use[0] is None:
                    wait(pe, nm_ready, turned)
                    return
                kind, g, n = bank_use[0]
                if kind == "q" and g >= B:
                    pe.wait_ge(sq_act, 2 * (g - B) + n + 1)
                elif kind == "n":
                    pe.wait_ge(n_act, 4 * (g - B) + n + 1)
                else:
                    reader = {"t": xnt_ready, "q": q_rest, "k": k_rest, "v": v_ready, "y": y_taken, "z": z_taken}
                    pe.wait_ge(reader[kind], 2 * g + n + 1)
                bank_use[0] = None

            def turn_maxima(pm, u):
                pe.wait_ge(mx_taken, 2 * TILES * pm + 2 * TILES)
                wait_bank(pm)
                nc.tensor.transpose(XB[0:2 * TILES, 0:128], NM[:, u, :], w["ident"]).then_inc(xb_full, 1)

            def scores(p, u, s, half):
                for hh in range(2):
                    j = 2 * half + hh
                    n = 4 * TILES * p + 4 * s + j
                    wait(pe, exp_done, n - 1)
                    nc.tensor.matmul(ST[:, j % 2, :], STK[:, u, s * 128:(s + 1) * 128],
                                     STQ[:, u, hh, half * HALF:(half + 1) * HALF],
                                     start=True, stop=True).then_inc(st_ready, 1)

            def values(p, u, s):
                pe.wait_ge(exp_done, 4 * TILES * p + 4 * s + 4)
                if s == 0:
                    wait(pe, evac, p)
                for j in range(4):
                    half, hh = j // 2, j % 2
                    g = 2 * hh + half
                    v = (hh * TILES + s) * VROW
                    last = nc.tensor.matmul(PV[32 * g:32 * g + VROW, :], VR[:, u, v:v + VROW],
                                            PT[:, s % 2, j, :], start=(s == 0), stop=(s == TILES - 1))
                last.then_inc(pv_done, 1)

            def pair(p, u, it, first=False, left=2):
                pe.wait_ge(ld_st[u], 80 * it + 80)
                pe.wait_ge(ld_m[u], 64 * it + 64)
                for s in range(TILES):
                    if s == TURN_STEP and left >= 1:
                        turn_maxima(p + 1, 1 - u)
                    scores(p, u, s, 0)
                    if s < TILES - AHEAD:
                        if left >= 1:
                            maxima(p + 1, 1 - u, s + AHEAD)
                    elif left >= 2:
                        maxima(p + 2, u, s - (TILES - AHEAD),
                               64 * it + 128 if s == TILES - AHEAD else None)
                    scores(p, u, s, 1)
                    if s > 0:
                        values(p, u, s - 1)
                    elif not first:
                        values(p - 1, 1 - u, TILES - 1)
                    for kind, g, n in extra_at(p, s):
                        wait_bank(min(p + 1 + (s >= TURN_STEP), ALL_PAIRS))
                        tile(kind, g, n, XB[:, :]).then_inc(xb_full, 1)
                        bank_use[0] = (kind, g, n)

            def body(it, first=False, last=False):
                pair(2 * it, 0, it, first, left=1 if last else 2)
                pair(2 * it + 1, 1, it, left=0 if last else 2)

            def tile(kind, g, n, to):
                layer = 1 if g < B else 2
                here = slice(n * HALF, (n + 1) * HALF)
                if kind == "t":
                    pe.wait_ge(xn_ready, g + 1)
                    for t in range(4):
                        last = nc.tensor.transpose(to[:, t * 128:(t + 1) * 128], XN[:, 4 * n + t, :], w["ident"])
                elif kind in ("q", "k"):
                    pe.wait_ge(xnt_ready, 2 * g + n + 1)
                    last = nc.tensor.matmul(to, w[f"{kind}{layer}"], XNT[:, here], start=True, stop=True)
                elif kind == "v":
                    pe.wait_ge(xnt_ready, 2 * g + n + 1)
                    for t in range(4):
                        k = 4 * n + t
                        last = nc.tensor.matmul(to[:, t * 128:(t + 1) * 128], XNT[:, k * 128:(k + 1) * 128],
                                                w[f"v{layer}"], start=True, stop=True)
                elif kind == "n":
                    pe.wait_ge(sq_act, 2 * (g - B) + n + 1)
                    last = nc.tensor.matmul(to, w["same_head"], SQ[:, here], start=True, stop=True)
                elif kind == "y":
                    pe.wait_ge(on_ready, g + 1)
                    for t in range(4):
                        k = 4 * n + t
                        last = nc.tensor.matmul(to[:, t * 128:(t + 1) * 128], ONN[:, k * 128:(k + 1) * 128],
                                                w["o1"], start=True, stop=True)
                else:
                    pe.wait_ge(on_ready, B + g + 1)
                    for t in range(3 * n, min(3 * n + 3, TILES)):
                        last = nc.tensor.matmul(to[:, t % 3 * OUTW:(t % 3 + 1) * OUTW],
                                                ONN[:, t * 128:(t + 1) * 128], w["p2"], start=True, stop=True)
                return last

            pe.wait_ge(w_loaded, 48)
            pe.wait_ge(scaled, 2)
            for kind, n in FIRST:
                tile(kind, 0, n, first_bank[kind, n]).then_inc(first_full, 1)
            for qt in range(TILES):
                maxima(0, 0, qt, 64 if qt == 0 else None)
            turn_maxima(0, 0)
            for qt in range(AHEAD):
                maxima(1, 1, qt, 64 if qt == 0 else None)
            for lo, hi in SPANS:
                if hi - lo == 1:
                    body(lo, first=lo == 0, last=hi == ITERATIONS)
                else:
                    wait_bank(2 * lo + 1)
                    with pe.Fori(lo, hi) as it:
                        body(it)
            values(ALL_PAIRS - 1, 1, TILES - 1)
            pe.wait_ge(exp_done, 4 * TILES * ALL_PAIRS)
            for n in range(3):
                tile("z", 1, n, last_bank[n]).then_inc(z_ready, 1)

        @block.scalar
        def _(act):
            def pair(p, u, it, first=False):
                for s in range(TILES):
                    step = TILES * p + s
                    for j in range(4):
                        n = 4 * step + j
                        act.wait_ge(st_ready, n + 1)
                        if j == 0:
                            wait(act, pv_done, step - 1)
                        nc.scalar.activation(PT[:, s % 2, j, :], ST[:, j % 2, :], ACT.Exp).then_inc(exp_done, 1)
                        if s == 1 and j == 1 and not first:
                            copy_out(p, 1 - u, 64 * (it - 1 + u))
                    for name, g, n in act_extras.pop((p, s), []) if isinstance(p, int) else []:
                        act_extra(name, g, n, p, s)

            def copy_out(pairs, u, stored):
                act.wait_ge(pv_done, TILES * pairs)
                wait(act, e_store[u], stored)
                nc.scalar.copy(E[:, u, :], PV[:, :]).then_inc(evac, 1)

            def body(it, first=False):
                pair(2 * it, 0, it, first)
                pair(2 * it + 1, 1, it)

            def act_extra(name, g, n, p, s, full=None):
                here = slice(n * HALF, (n + 1) * HALF)
                layer = 1 if g < B else 2
                src = XB[:, :]
                if full is not None:
                    src = first_bank[name, n] if len(name) == 1 else None
                    if src is not None:
                        act.wait_ge(first_full, full + 1)
                elif len(name) == 1:
                    act.wait_ge(xb_full, xb_use(p, s) + 1)
                if name == "t":
                    nc.scalar.copy(XNT[:, here], src).then_inc(xnt_ready, 1)
                elif name in ("q", "k"):
                    if n == 0 and g == 1:
                        act.wait_ge(first_main, MAIN)
                        act.wait_ge(first_rest, REST)
                    elif n == 0 and g > 1:
                        act.wait_ge(main_stored, MAIN * (g - 1))
                        act.wait_ge(rest_stored, REST * (g - 1))
                    if name == "k":
                        nc.scalar.activation(KB[:, 2, here], src, ACT.Identity, bias=col[f"bk{layer}"])\
                          .then_inc(k_first, 1)
                    elif layer == 1:
                        nc.scalar.activation(QB[:, 0, here], src, ACT.Identity, bias=qbias[:, :])\
                          .then_inc(q_first, 1)
                    else:
                        nc.scalar.activation(QT[:, here], src, ACT.Identity, bias=col["bq2"]).then_inc(q_first, 1)
                        nc.scalar.activation(SQ[:, here], src, ACT.Square, bias=col["bq2"]).then_inc(sq_act, 1)
                elif name == "q second":
                    act.wait_ge(q_rest, 2 * g + n + 1)
                    nc.scalar.copy(QB[:, 1, here], QR[:, here]).then_inc(q_second, 1)
                elif name == "k second":
                    act.wait_ge(k_rest, 2 * g + n + 1)
                    nc.scalar.copy(KB[:, 1, here], KR[:, here]).then_inc(k_second, 1)
                elif name == "n":
                    nc.scalar.copy(N2[:, here], src).then_inc(n_act, 1)
                elif name == "rsqrt":
                    r = g - B
                    act.wait_ge(n_act, 4 * r + 2)
                    nc.scalar.activation(LN2[:, :], N2[:, :], ACT.Ln).then_inc(n_act, 1)
                    act.wait_ge(n_act, 4 * r + 3)
                    nc.scalar.activation(Y[:, :], LN2[:, :], ACT.Exp, scale=-0.5).then_inc(n_act, 1)
                elif name == "gates":
                    gates(g)

            def gates(b):
                act.wait_ge(g_dve, G_STEPS * b + G_BEFORE)
                nc.scalar.activation(GE[:, :, :], GL[:, :, :], ACT.Exp).then_inc(g_act, 1)

            act.wait_ge(small_ready, 2)
            nc.scalar.activation(soft[:, 1:2], soft[:, 0:1], ACT.Exp, scale=-1.0).then_inc(small_act, 1)
            act.wait_ge(small_act, 1)
            nc.scalar.activation(soft[:, 2:3], soft[:, 1:2], ACT.Ln, bias=1.0).then_inc(small_act, 1)
            for full, (kind, n) in enumerate(FIRST):
                if kind in ("t", "q", "k"):
                    act_extra(kind, 0, n, None, None, full)
                if (kind, n) == ("k", 0):
                    act_extra("q second", 0, 0, None, None, full)
                if (kind, n) == ("k", 1):
                    for name, m in (("k second", 0), ("q second", 1), ("k second", 1)):
                        act_extra(name, 0, m, None, None, full)
            act_extras = {}
            for (p, s), (kind, g, n) in sorted(EXTRA.items()):
                after = (p + (s + 1) // TILES, (s + 1) % TILES)
                if kind in ("t", "q", "k", "n"):
                    act_extras.setdefault((p, s), []).append((kind, g, n))
                if kind == "k" or (kind == "q" and g < B):
                    act_extras.setdefault(after, []).append((kind + " second", g, n))
                if kind == "n" and n == 1:
                    act_extras.setdefault(after, []).append(("rsqrt", g, n))
                if kind == "z" and n == 2:
                    act_extras.setdefault(after, []).append(("gates", g, n))
            for lo, hi in SPANS:
                if hi - lo == 1:
                    body(lo, first=lo == 0)
                else:
                    with act.Fori(lo, hi) as it:
                        body(it)
            assert not act_extras
            copy_out(ALL_PAIRS, 1, 64 * (ALL_PAIRS // 2 - 1))
            gates(1)

        @block.vector
        def _(dve):
            def maximum(pm, u, qt):
                for hh in range(2):
                    dve.wait_ge(mx_ready, 2 * TILES * pm + 2 * qt + hh + 1)
                    c = hh * TILES + qt
                    nc.vector.tensor_reduce(NM[:, u, c:c + 1], MX[:, hh, :], AX.X, ALU.max, negate=True)\
                      .then_inc(mx_taken, 1)

            def split_maxima(pm, u, stored, use):
                dve.wait_ge(xb_full, use + 1)
                wait(dve, ld_m[u], stored)
                nc.vector.tensor_copy(NB[:, u, 0, :], XB[0:2 * TILES, 0:128]).then_inc(nm_first, 1)
                dve.wait_ge(nm_first, pm + 1)
                nc.vector.tensor_tensor(NB[:, u, 1, :], XB[0:2 * TILES, 0:128], NB[:, u, 0, :], ALU.subtract)\
                  .then_inc(nm_ready, 1)

            def pair(p, u, it, extras, left=2):
                for s in range(TILES):
                    if s == TURN_STEP and left >= 1:
                        split_maxima(p + 1, 1 - u, 64 * (it + u), p + 1 + extras)
                    if s < TILES - AHEAD:
                        if left >= 1:
                            maximum(p + 1, 1 - u, s + AHEAD)
                    elif left >= 2:
                        maximum(p + 2, u, s - (TILES - AHEAD))
                    if s == SUMS_STEP and isinstance(p, int) and p in SUMS_AT:
                        reciprocals(SUMS_AT.index(p))
                    for kind, g, n in extra_at(p, s):
                        use = xb_use(p, s)
                        extras += 1
                        if kind in ("q", "k", "v", "y", "z"):
                            dve_extra(kind, g, n, XB[:, :], use)
                        if kind == "y" and n == 1:
                            norm(g + B, g)
                        if kind == "z" and n == 2:
                            gates(0)

            def body(it, extras, last=False):
                pair(2 * it, 0, it, extras, left=1 if last else 2)
                if isinstance(it, int):
                    extras = extras_before(2 * it + 1)
                pair(2 * it + 1, 1, it, extras, left=0 if last else 2)

            def dve_extra(kind, g, n, src, use=None, full=None):
                layer = 1 if g < B else 2
                here = slice(n * HALF, (n + 1) * HALF)
                if kind in ("q", "k"):
                    if kind == "q" and layer == 2:
                        return
                    dve.wait_ge(q_first if kind == "q" else k_first, 2 * g + n + 1)
                    rest, part = (QR, QB[:, 0, here]) if kind == "q" else (KR, KB[:, 2, here])
                    bias = qbias[:, :] if kind == "q" else col[f"bk{layer}"]
                    nc.vector.scalar_tensor_tensor(rest[:, here], src, bias, part, ALU.add, ALU.subtract)\
                      .then_inc(q_rest if kind == "q" else k_rest, 1)
                    return
                if full is None:
                    dve.wait_ge(xb_full, use + 1)
                else:
                    dve.wait_ge(first_full, full + 1)
                if kind == "v":
                    for t in range(4):
                        where = VA[:, PAIRS * g:PAIRS * (g + 1), :]\
                            .rearrange("p j (e k d) -> p j e k d", e=2, k=TILES)[:, :, :, 4 * n + t, 0:DH]\
                            .rearrange("p j e d -> p (j e) d")
                        last = nc.vector.tensor_tensor(
                            where, src[:, t * 128:(t + 1) * 128].rearrange("p (h d) -> p h d", d=DH),
                            row[f"bv{layer}"].rearrange("p (h d) -> p h d", d=DH), ALU.add)
                    last.then_inc(v_ready, 1)
                elif kind == "y":
                    dve.wait_ge(biased, g + 1)
                    Xh = X[:, g, 4 * n:4 * n + 4, :].rearrange("p t c -> p (t c)")
                    nc.vector.tensor_tensor(Xh, src, Xh, ALU.add).then_inc(y_taken, 1)
                elif kind == "z":
                    take_z(n, src)

            def take_z(n, src):
                m = min(3, TILES - 3 * n)
                return nc.vector.tensor_copy(Z[:, 3 * n:3 * n + m, :],
                                             src[:, 0:m * OUTW].rearrange("p (t c) -> p t c", t=m))\
                         .then_inc(z_taken, 1)

            def norm(g, b):
                wait(dve, xn_ready, g)
                if g >= B:
                    dve.wait_ge(y_taken, 2 * b + 2)
                for t in range(TILES):
                    last = nc.vector.bn_stats(stats[:, t, :], X[:, b, t, :])
                last.then_inc(stats_dve, 1)
                dve.wait_ge(stats_dve, 2 * g + 1)
                for t in range(TILES):
                    last = nc.vector.bn_aggr(mv[:, t, :], stats[:, t, :])
                last.then_inc(stats_dve, 1)
                dve.wait_ge(stats_dve, 2 * g + 2)
                nc.vector.tensor_scalar(var[:, :], mv[:, :, 1], EPS, None, ALU.add).then_inc(var_ready, 1)

            def reciprocals(e):
                dve.wait_ge(dc_loaded, 16 * e + 16)
                nc.vector.reciprocal(RC[:, :], DC[:, :]).then_inc(dc_ready, 1)

            def gates(b):
                steps = [0]

                def then(ins):
                    steps[0] += 1
                    ins.then_inc(g_dve, 1)
                    dve.wait_ge(g_dve, G_STEPS * b + steps[0])

                if b == 1:
                    for n in range(3):
                        dve.wait_ge(z_ready, n + 1)
                        take_z(n, last_bank[n])
                dve.wait_ge(z_taken, 3 * b + 3)
                then(nc.vector.tensor_tensor(GL[:, :, :], Z[:, :, D:OUTW],
                                             row["brs"].unsqueeze(1).to_broadcast([128, TILES, NG + 2]), ALU.add))
                part = [slice(0, NG), slice(NG, NG + 2)]
                for i in range(2):
                    then(nc.vector.tensor_reduce(GM[:, i, :], GL[:, :, part[i]], AX.X, ALU.max))
                for i in range(2):
                    n = part[i].stop - part[i].start
                    then(nc.vector.tensor_tensor(GL[:, :, part[i]], GL[:, :, part[i]],
                                                 GM[:, i, :].unsqueeze(2).to_broadcast([128, TILES, n]),
                                                 ALU.subtract))
                assert steps[0] == G_BEFORE
                dve.wait_ge(g_act, b + 1)
                for t in range(TILES):
                    last = nc.vector.max(T8[:, t, :], GE[:, t, 0:NG])
                then(last)
                for i in range(2):
                    then(nc.vector.tensor_reduce(GS[:, i, :], GE[:, :, part[i]], AX.X, ALU.add))
                then(nc.vector.reciprocal(GR[:, :, :], GS[:, :, :]))
                then(nc.vector.tensor_reduce(G3[:, 0, :], T8[:, :, 0:TOP], AX.X, ALU.add))
                then(nc.vector.tensor_tensor(G3[:, 0, :], G3[:, 0, :], GR[:, 0, :], ALU.mult))
                then(nc.vector.tensor_tensor(SW[:, :, :], GE[:, :, part[1]],
                                             GR[:, 1, :].unsqueeze(2).to_broadcast([128, TILES, 2]), ALU.mult))
                then(nc.vector.tensor_tensor(G3[:, 1, :], SW[:, :, 0], SW[:, :, 1], ALU.add))
                then(nc.vector.tensor_tensor(G3[:, 1, :], G3[:, 1, :], SW[:, :, 0], ALU.mult))
                then(nc.vector.tensor_tensor(G3[:, 2, :], G3[:, 0, :], SW[:, :, 1], ALU.mult))
                then(nc.vector.tensor_scalar(G3[:, 1, :], G3[:, 1, :], 2.0, None, ALU.mult))
                then(nc.vector.tensor_scalar(G3[:, 2, :], G3[:, 2, :], 2.0 * TOP, None, ALU.mult))
                then(nc.vector.tensor_tensor(gate[:, :], G3[:, 1, :], G3[:, 2, :], ALU.add))
                dve.wait_ge(biased, B + b + 1)
                for t in range(TILES):
                    last = nc.vector.scalar_tensor_tensor(X[:, b, t, :], Z[:, t, 0:D], gate[:, t:t + 1],
                                                          X[:, b, t, :], ALU.mult, ALU.add)
                last.then_inc(out_ready, 1)
                assert steps[0] == G_STEPS, steps[0]

            nc.vector.memset(STK[:, :, :], 1.0).then_inc(fill_ready, 1)
            for tile in (MXQ, MXK, STQ):
                nc.vector.memset(tile[:].bitcast(F32), 0.0).then_inc(fill_ready, 1)
            nc.vector.memset(half_neg[:, :], -0.5).then_inc(small_ready, 1)
            dve.wait_ge(x_loaded[0], 16)
            norm(0, 0)
            dve.wait_ge(w_loaded, 48)
            nc.vector.tensor_scalar(w["q1"], w["q1"], DH ** -0.5, None, ALU.mult).then_inc(scaled, 1)
            nc.vector.tensor_scalar(qbias[:, :], col["bq1"], DH ** -0.5, None, ALU.mult).then_inc(scaled, 1)
            dve.wait_ge(scaled, 2)
            nc.vector.scalar_tensor_tensor(soft[:, 0:1], col["temp"], -1.0, col["temp"], ALU.mult, ALU.max)\
              .then_inc(small_ready, 1)
            for full, (kind, n) in enumerate(FIRST):
                if kind in ("q", "k"):
                    dve_extra(kind, 0, n, first_bank[kind, n], full=full)
            dve.wait_ge(ones_ready, 1)
            for full, (kind, n) in enumerate(FIRST):
                if kind == "v":
                    dve_extra(kind, 0, n, first_bank[kind, n], full=full)
            dve.wait_ge(v_ready, 2)
            nc.vector.memset(PV[:, :], 0.0).then_inc(pv_zero, 1)
            dve.wait_ge(small_act, 2)
            nc.vector.scalar_tensor_tensor(head_scale[:, :], col["temp"], 0.0, soft[:, 2:3], ALU.max, ALU.add)\
              .then_inc(small_ready, 1)
            dve.wait_ge(small_ready, 3)
            nc.vector.tensor_scalar(head_scale[:, :], head_scale[:, :], DH ** -0.5, None, ALU.mult)\
              .then_inc(small_ready, 1)
            dve.wait_ge(x_loaded[1], 16)
            norm(1, 1)
            for qt in range(TILES):
                maximum(0, 0, qt)
            split_maxima(0, 0, 0, 0)
            for qt in range(AHEAD):
                maximum(1, 1, qt)
            for lo, hi in SPANS:
                extras = extras_before(2 * lo)
                if hi - lo == 1:
                    body(lo, extras, last=hi == ITERATIONS)
                else:
                    with dve.Fori(lo, hi) as it:
                        body(it, extras)
            dve.wait_ge(on_loaded, 3 * 32 + 64)
            nc.vector.reciprocal(RDEN[:, :], DEN[:, :]).then_inc(last_dve, 1)
            dve.wait_ge(last_dve, 1)
            nc.vector.tensor_tensor(ONN[:, :], ON[:, :], RDEN[:, :], ALU.mult).then_inc(on_ready, 1)
            gates(1)

        @block.gpsimd
        def _(pool):
            nc.gpsimd.memset(VA[:, :, :], 1.0).then_inc(ones_ready, 1)

            def norm(g, b):
                pool.wait_ge(var_ready, g + 1)
                nc.gpsimd.tensor_tensor(rstd[:, :], var[:, :], half_neg[:, :], ALU.pow).then_inc(ln_pool, 1)
                pool.wait_ge(ln_pool, 2 * g + 1)
                nc.gpsimd.tensor_tensor(shift[:, :], mv[:, :, 0], rstd[:, :], ALU.mult).then_inc(ln_pool, 1)
                pool.wait_ge(ln_pool, 2 * g + 2)
                wait(pool, xnt_ready, 2 * g)
                for t in range(TILES):
                    last = nc.gpsimd.tensor_scalar(XN[:, t, :], X[:, b, t, :], rstd[:, t:t + 1],
                                                   shift[:, t:t + 1], ALU.mult, ALU.subtract)
                last.then_inc(xn_ready, 1)

            def third(g, layer):
                if layer == 1:
                    pool.wait_ge(q_second, 2 * g + 2)
                    nc.gpsimd.tensor_tensor(QB[:, 2, :], QR[:, :], QB[:, 1, :], ALU.subtract).then_inc(q_third, 1)
                pool.wait_ge(k_second, 2 * g + 2)
                nc.gpsimd.tensor_tensor(KB[:, 0, :], KR[:, :], KB[:, 1, :], ALU.subtract).then_inc(k_third, 1)

            def store(g, q):
                store_main(pool, g, q)
                store_rest(pool, g, q)

            def queries2(g):
                k = [9 * (g - B)]

                def then(ins):
                    k[0] += 1
                    ins.then_inc(q_pool, 1)
                    pool.wait_ge(q_pool, k[0])

                pool.wait_ge(n_act, 4 * (g - B) + 4)
                then(nc.gpsimd.tensor_tensor(LN2[:, :], Y[:, :], Y[:, :], ALU.mult))
                then(nc.gpsimd.tensor_tensor(LN2[:, :], LN2[:, :], N2[:, :], ALU.mult))
                then(nc.gpsimd.tensor_scalar(LN2[:, :], LN2[:, :], -0.5, 1.5, ALU.mult, ALU.add))
                then(nc.gpsimd.tensor_tensor(Y[:, :], Y[:, :], LN2[:, :], ALU.mult))
                then(nc.gpsimd.tensor_tensor(QT[:, :], QT[:, :], Y[:, :], ALU.mult))
                then(nc.gpsimd.tensor_scalar(QT[:, :], QT[:, :], col["qe"], head_scale[:, :], ALU.add, ALU.mult))
                then(nc.gpsimd.tensor_scalar(QB[:, 0, :], QT[:, :], 1.0, 1.0, ALU.mult, ALU.mult))
                then(nc.gpsimd.tensor_tensor(QR[:, :], QT[:, :], QB[:, 0, :], ALU.subtract))
                then(nc.gpsimd.tensor_scalar(QB[:, 1, :], QR[:, :], 1.0, 1.0, ALU.mult, ALU.mult))
                nc.gpsimd.tensor_tensor(QB[:, 2, :], QR[:, :], QB[:, 1, :], ALU.subtract).then_inc(q_third, 1)
                pool.wait_ge(q_third, g + 1)

            def add_bias(b, layer):
                pool.wait_ge(xn_ready, B * (layer - 1) + b + 1)
                nc.gpsimd.tensor_tensor(X[:, b], X[:, b], row["bo1" if layer == 1 else "bp"].unsqueeze(1)
                                        .to_broadcast([128, TILES, D]), ALU.add).then_inc(biased, 1)

            def reload(e):
                for u in range(2):
                    pool.wait_ge(e_store[u], 256 * e + 256)
                wait(pool, on_ready, e)
                for qh in range(2):
                    here = slice(qh * HALF, (qh + 1) * HALF)
                    src = os_[H * e:H * (e + 1), qh]
                    pool.dma_start(ON[:, here], src[:, 0:DH, :]).then_inc(on_loaded, 16)
                    if e == SEGMENTS - 1:
                        pool.dma_start(DEN[:, here], src[:, DH:VROW, :].to_broadcast([H, DH, HALF]))\
                            .then_inc(on_loaded, 16)

            def divide(e):
                heads = slice(H * e, H * (e + 1))
                pool.dma_start(DC[:, :], os_[heads, :, DH, :].rearrange("h a (k n) -> (h a) k n", n=128))\
                    .then_inc(dc_loaded, 16)
                pool.wait_ge(dc_ready, e + 1)
                pool.dma_start(rs_[heads].rearrange("h (k n) -> (h k) n", n=128), RC[:, :]).then_inc(rc_stored, 16)
                pool.wait_ge(rc_stored, 16 * e + 16)
                pool.dma_start(RDEN[:, :], rs_[heads].unsqueeze(1).to_broadcast([H, DH, S])).then_inc(r_loaded, 16)
                pool.wait_ge(r_loaded, 16 * e + 16)
                pool.wait_ge(on_loaded, 32 * e + 32)
                nc.gpsimd.tensor_tensor(ONN[:, :], ON[:, :], RDEN[:, :], ALU.mult).then_inc(on_ready, 1)

            norm(0, 0)
            pool.wait_ge(w_loaded, 48)
            third(0, 1)
            norm(1, 1)
            for b in range(B):
                add_bias(b, 1)
            third(1, 1)
            pool.wait_ge(q_third, 2)
            store(1, True)
            pool.wait_ge(k_third, 2)
            store(1, False)
            for b in range(B):
                reload(b)
                divide(b)
                norm(B + b, b)
                add_bias(b, 2)
                queries2(B + b)
                store(B + b, True)
                third(B + b, 2)
                pool.wait_ge(k_third, B + b + 1)
                store(B + b, False)
            reload(2)
            divide(2)
            reload(3)


_INS = ["x", "wmat", "wcol", "wrow"]


def kernel(**inputs):
    import numpy as np
    import concourse.bacc as bacc
    from concourse.bass_utils import run_bass_kernel_spmd

    a = {n: np.asarray(v) for n, v in inputs.items()}
    L1 = {n: a["L0_attn_" + n] for n in ("x", "Wq", "bq", "Wk", "bk", "Wv", "bv", "Wo", "bo")}
    L2 = {n: a["L0_ffn_" + n] for n in ("Wq", "bq", "Wk", "bk", "Wv", "bv", "Wp", "bp", "Wr", "br", "Ws", "bs",
                                         "temperature", "query_embedding")}
    f = np.float32
    eye = np.eye(D, dtype=f)
    heads = np.kron(np.eye(H, dtype=f), np.ones((DH, DH), f))
    arrays = {
        "x": np.ascontiguousarray(L1["x"].reshape(B * S, D)),
        "wmat": np.ascontiguousarray(np.concatenate(
            [L1["Wq"].T, L1["Wk"].T, L1["Wv"].T, L1["Wo"].T, L2["Wq"].T, L2["Wk"].T, L2["Wv"].T,
             L2["Wp"].T, L2["Wr"].T, L2["Ws"].T, eye, heads], axis=1)),
        "wcol": np.ascontiguousarray(np.stack(
            [L1["bq"], L1["bk"], L2["bq"], L2["bk"], L2["query_embedding"].reshape(D),
             np.repeat(L2["temperature"].reshape(H), DH)], axis=1)),
        "wrow": np.ascontiguousarray(np.concatenate(
            [L1["bv"], L1["bo"], L2["bv"], L2["bp"], L2["br"], L2["bs"]]).reshape(1, R_WIDTH)),
    }
    nc = bacc.Bacc("TRN2", target_bir_lowering=False, num_devices=1)
    args = [nc.dram_tensor(n, arrays[n].shape, F32, kind="ExternalInput").ap() for n in _INS]
    args.append(nc.dram_tensor("out", (B * S, D), F32, kind="ExternalOutput").ap())
    args.append(nc.dram_tensor("q_parts", (COMBOS, SEGMENTS * D, S), BF16).ap())
    args.append(nc.dram_tensor("k_parts", (COMBOS, SEGMENTS * D, S), BF16).ap())
    args.append(nc.dram_tensor("head_sums", (SEGMENTS * H, 2, VROW, HALF), F32).ap())
    args.append(nc.dram_tensor("reciprocals", (SEGMENTS * H, S), F32).ap())
    moe_attention_program(nc, *args)
    r = run_bass_kernel_spmd(nc, [arrays], core_ids=[0])
    return np.asarray(r.results[0]["out"]).reshape(B, S, D)
```

```python
import concourse.bass as bass
from concourse import mybir
from contextlib import ExitStack

F32 = mybir.dt.float32
BF16 = mybir.dt.bfloat16
ALU = mybir.AluOpType
ACT = mybir.ActivationFunctionType
AX = mybir.AxisListType

B, S, D, H = 2, 1024, 128, 16
DH = D // H
TILES = S // 128
HALF = 512
PAIRS = H // 2
SEGMENTS = 2 * B
ALL_PAIRS = SEGMENTS * PAIRS
NG = H - 1
TOP = 3
EPS = 1e-5

COMBOS = 6
CROWS = COMBOS * DH
MROWS = 3 * DH
MAIN_PARTS = {"q": (0, 0, 1), "k": (1, 0, 0)}
VROW = DH + 1
VPAIR = 2 * TILES * VROW
TURN_STEP = 5
AHEAD = 4
FIRST_AHEAD = 3
FIRST_STEPS = {0: (1,) * TILES, 1: (1, 1, 1, 1, 1, 1, 2, 1)}

W_COLS = {}
_at = 0
for _name, _n in (("q1", D), ("k1", D), ("v1", D), ("o1", D), ("q2", D), ("k2", D), ("v2", D),
                  ("p2", D + NG + 2), ("ident", D), ("heads", H), ("sums", 4)):
    W_COLS[_name] = (_at, _at + _n)
    _at += _n
W_WIDTH = _at
COLS = ["bq1", "bk1", "bq2", "bk2", "qe", "temp"]
R_COLS = {}
_at = 0
for _name, _n in (("bv1", D), ("bo1", D), ("bv2", D), ("bp", D), ("brs", NG + 2)):
    R_COLS[_name] = (_at, _at + _n)
    _at += _n
R_WIDTH = _at
OUTW = D + NG + 2
LAST = D - 2 * DH


EXTRA = {}


def _plan():
    def put(at, kind, g, n):
        EXTRA[at] = (kind, g, n)

    for b in range(B):
        p = PAIRS * (b + 1) + 1
        for s, kind, n in ((2, "y", 0), (3, "y", 1), (8, "t", 0), (9, "t", 1), (10, "q", 0), (11, "q", 1),
                           (13, "n", 0), (14, "k", 0), (16, "k", 1), (18, "v", 0), (19, "v", 1),
                           (21, "r", 0), (24, "r", 1)):
            put((p + s // TILES, s % TILES), kind, b if kind == "y" else B + b, n)
    for n, s in enumerate((5, 6, 7)):
        put((ALL_PAIRS - 2, s), "z", 0, n)


_plan()
SUMS_STEP, SUMS_AT = 6, [PAIRS, 2 * PAIRS, 3 * PAIRS]


def later(p, s, steps):
    return (p + (s + steps) // TILES, (s + steps) % TILES)


def at_step(work, p, s):
    return work.get((p, s), []) if isinstance(p, int) else []


def extra_at(p, s):
    return [EXTRA[p, s]] if isinstance(p, int) and (p, s) in EXTRA else []


def extras_before(p, s=0):
    return sum(at < (p, s) for at in EXTRA)


def last_tile(p, s, turning=False):
    if not isinstance(p, int):
        return None
    turned = (p if s >= TURN_STEP and not turning else p - 1, TURN_STEP)
    return EXTRA.get(max((at for at in EXTRA if turned <= at < (p, s)), default=None))


def due(p, s):
    if not isinstance(p, int) or p not in FIRST_STEPS:
        return [(1 + (s + AHEAD) // TILES, (s + AHEAD) % TILES)]
    done = FIRST_AHEAD + sum(sum(FIRST_STEPS[q]) - TILES for q in range(p)) + sum(FIRST_STEPS[p][:s])
    return [(1 + i // TILES, i % TILES) for i in range(done, done + FIRST_STEPS[p][s])]


def moe_attention_program(nc, x, wmat, wcol, wrow, out, qc, kc, os_, rs_):
    ctx = ExitStack()
    with ctx:
        def sb(name, shape, dt=F32):
            return ctx.enter_context(nc.sbuf_tensor(name, shape, dt))

        def sem(name):
            return ctx.enter_context(nc.semaphore(name))

        X = sb("X", [128, B, TILES, D])
        W = sb("W", [128, W_WIDTH])
        C = sb("C", [128, len(COLS)])
        R = sb("R", [128, R_WIDTH])
        col = {n: C[:, i:i + 1] for i, n in enumerate(COLS)}
        w = {n: W[:, a:b] for n, (a, b) in W_COLS.items()}
        row = {n: R[:, a:b] for n, (a, b) in R_COLS.items()}
        qbias = sb("qbias", [128, 1])
        head_scale = sb("head_scale", [128, 1])
        soft = sb("soft", [128, 3])
        stats = sb("stats", [128, TILES, 6])
        mv = sb("mv", [128, TILES, 2])
        var = sb("var", [128, TILES])
        half_neg = sb("half_neg", [128, TILES * H])
        rstd = sb("rstd", [128, TILES])
        neg_mean = sb("neg_mean", [128, TILES])
        shift = sb("shift", [128, TILES])
        XN = sb("XN", [128, TILES, D])
        XNT = sb("XNT", [128, S])
        QT = sb("QT", [128, S])
        QR = sb("QR", [128, S])
        KR = sb("KR", [128, S])
        QB = sb("QB", [128, 3, S], BF16)
        KB = sb("KB", [128, 3, S], BF16)
        SQ = sb("SQ", [128, S])
        KT = sb("KT", [128, S])
        VT = sb("VT", [128, S])
        N2 = sb("N2", [128, TILES * H])
        RN = sb("RN", [128, TILES * H])
        RH = sb("RH", [128, S])
        VA = sb("VA", [128, ALL_PAIRS, VPAIR])
        STQ = sb("STQ", [128, 2, 2, S], BF16)
        STK = sb("STK", [128, 2, S], BF16)
        MXQ = sb("MXQ", [128, 2, 2, S], BF16)
        MXK = sb("MXK", [128, 2, S], BF16)
        VR = sb("VR", [128, 2, VPAIR])
        NM = sb("NM", [128, 2, 2 * TILES])
        NB = sb("NB", [2 * TILES, 2, 2, 128], BF16)
        PT = sb("PT", [128, 2, 4, HALF])
        E = sb("E", [128, 2, HALF])
        ON = sb("ON", [128, S])
        DEN = sb("DEN", [128, S])
        DC = sb("DC", [128, 128])
        RC = sb("RC", [128, 128])
        RDEN = sb("RDEN", [128, S])
        WL = sb("WL", [128, 2, 2 * OUTW + 2])
        RS = sb("RS", [128, TILES, 2])
        ONN = sb("ONN", [128, S])
        Z = sb("Z", [128, TILES, OUTW])
        GL = sb("GL", [128, TILES, NG + 2])
        GE = sb("GE", [128, TILES, NG + 2])
        GM = sb("GM", [128, 2, TILES])
        T8 = sb("T8", [128, TILES, 8])
        GS = sb("GS", [128, 2, TILES])
        GR = sb("GR", [128, 2, TILES])
        G3 = sb("G3", [128, 3, TILES])
        SW = sb("SW", [128, TILES, 2])
        gate = sb("gate", [128, TILES])

        ST = ctx.enter_context(nc.psum_tensor("ST", [128, 2, HALF], F32))
        MX = ctx.enter_context(nc.psum_tensor("MX", [128, 2, 2 * HALF], F32))
        PV = ctx.enter_context(nc.psum_tensor("PV", [128, HALF], F32))
        XB = ctx.enter_context(nc.psum_tensor("XB", [128, HALF], F32))
        last_bank = [XB[:, :], MX[:, 0, 0:HALF], MX[:, 0, HALF:]]
        pair_bank = [ST[:, 0, :], ST[:, 1, :], MX[:, 1, 0:HALF], MX[:, 1, HALF:], PV[:, :], *last_bank]
        wide_bank = [ST[:, 0, :], ST[:, 1, :], MX[:, 0, 0:HALF], MX[:, 0, HALF:]]
        first_bank = {("t", 0, 0): ST[:, 0, :], ("t", 0, 1): ST[:, 1, :],
                      ("q", 0, 0): MX[:, 0, 0:HALF], ("k", 0, 0): MX[:, 1, 0:HALF],
                      ("q", 0, 1): MX[:, 0, HALF:], ("k", 0, 1): MX[:, 1, HALF:],
                      ("v", 0, 0): XB[:, :], ("v", 0, 1): PV[:, :],
                      ("t", 1, 0): ST[:, 0, :], ("t", 1, 1): ST[:, 1, :],
                      ("q", 1, 0): PV[:, :], ("q", 1, 1): XB[:, :],
                      ("k", 1, 0): ST[:, 0, :], ("k", 1, 1): ST[:, 1, :],
                      ("v", 1, 0): PV[:, :], ("v", 1, 1): ST[:, 0, :]}
        FIRST = list(first_bank)
        BETWEEN = {2: FIRST[8:10], 3: FIRST[10:11], 4: FIRST[11:13], 5: FIRST[13:14], 6: FIRST[14:15], 7: FIRST[15:]}

        x_loaded = [sem(f"x_loaded{b}") for b in range(B)]
        w_loaded = sem("w_loaded")
        ones_ready = sem("ones_ready")
        fill_ready = sem("fill_ready")
        ld_queries = sem("ld_queries")
        ld_first = sem("ld_first")
        scaled = sem("scaled")
        pv_zero = sem("pv_zero")
        small_act = sem("small_act")
        small_ready = sem("small_ready")
        ld_mx = [sem(f"ld_mx{u}") for u in range(2)]
        ld_st = [sem(f"ld_st{u}") for u in range(2)]
        ld_m = [sem(f"ld_m{u}") for u in range(2)]
        st_ready, exp_done = sem("st_ready"), sem("exp_done")
        mx_ready, mx_taken = sem("mx_ready"), sem("mx_taken")
        nm_first, nm_ready = sem("nm_first"), sem("nm_ready")
        pv_done, evac = sem("pv_done"), sem("evac")
        e_store = [sem(f"e_store{u}") for u in range(2)]
        first_full = sem("first_full")
        xb_full = sem("xb_full")
        stats_dve, var_ready, ln_pool = sem("stats_dve"), sem("var_ready"), sem("ln_pool")
        xn_first, xn_ready = sem("xn_first"), sem("xn_ready")
        q_full, k_full, v_full = sem("q_full"), sem("k_full"), sem("v_full")
        xnt_ready = sem("xnt_ready")
        q_first, q_rest, q_second = sem("q_first"), sem("q_rest"), sem("q_second")
        k_first, k_rest, k_second = sem("k_first"), sem("k_rest"), sem("k_second")
        v_ready, sq_act, n_act = sem("v_ready"), sem("sq_act"), sem("n_act")
        rn_ready, q_normed = sem("rn_ready"), sem("q_normed")
        q_third, k_third, q_pool = sem("q_third"), sem("k_third"), sem("q_pool")
        first_main, first_rest = sem("first_main"), sem("first_rest")
        main_stored, rest_stored = sem("main_stored"), sem("rest_stored")
        on_loaded, dc_loaded, dc_ready, rc_stored, r_loaded = (sem("on_loaded"), sem("dc_loaded"),
                                                               sem("dc_ready"), sem("rc_stored"), sem("r_loaded"))
        on_ready = sem("on_ready")
        wl_zero, wl_sums, wl_loaded = sem("wl_zero"), sem("wl_sums"), sem("wl_loaded")
        last_loaded = [sem(f"last_loaded{half}") for half in range(2)]
        last_inverse, last_ready = sem("last_inverse"), sem("last_ready")
        pair_ready, rs_ready, pair_added = sem("pair_ready"), sem("rs_ready"), sem("pair_added")
        biased, y_taken = sem("biased"), sem("y_taken")
        z_ready, z_taken = sem("z_ready"), sem("z_taken")
        g_dve, g_act, out_ready, out_stored = sem("g_dve"), sem("g_act"), sem("out_ready"), sem("out_stored")

        ITERATIONS = ALL_PAIRS // 2
        own = {0, ITERATIONS - 1} | {p // 2 for p, s in EXTRA} | {p // 2 for p in SUMS_AT}
        SPANS = []
        for it in range(ITERATIONS):
            if it in own or it - 1 in own:
                SPANS.append((it, it + 1))
            else:
                SPANS[-1] = (SPANS[-1][0], it + 1)

        def xb_use(p, s):
            return p + 1 + extras_before(p, s) + (s >= TURN_STEP)

        G_STEPS, G_BEFORE = 18, 5
        block = ctx.enter_context(nc.Block())

        def wait(eng, s, value):
            if not isinstance(value, int) or value > 0:
                eng.wait_ge(s, value)

        def values_of(g, t):
            return VA[:, PAIRS * g:PAIRS * (g + 1), :].rearrange("p j (e k d) -> p j e k d", e=2, k=TILES)\
                [:, :, :, t, 0:DH].rearrange("p j e d -> p (j e) d")

        def wide(p, s):
            return isinstance(p, int) and (p, s) >= (ALL_PAIRS - 2, TURN_STEP)

        def score_bank(p, s, j):
            return wide_bank[j] if wide(p, s) else ST[:, j % 2, :]

        def load_first(eng, kind, part):
            for c in range(3):
                for hh in range(2):
                    if MAIN_PARTS[kind][c] == part:
                        rows = slice(64 * hh + DH * c, 64 * hh + DH * (c + 1))
                        head = slice(DH * hh, DH * (hh + 1))
                        to, source = ((MXQ[rows, 0, hh, :], QB[head, part, :]) if kind == "q" else
                                      (MXK[rows, 0, :], KB[head, 2 - part, :]))
                        eng.dma_start(to, source).then_inc(ld_queries if (kind, part) == ("q", 0) else ld_first, 16)

        def store_main(eng, g, q=True):
            for c, part in enumerate(MAIN_PARTS["q" if q else "k"]):
                eng.dma_start((qc if q else kc)[c, D * g:D * (g + 1), :], QB[:, part, :] if q else KB[:, 2 - part, :])\
                   .then_inc(main_stored if g else first_main, 16)

        def store_rest(eng, g, q=True):
            scratch, B3 = (qc, QB) if q else (kc, KB)
            eng.dma_start(scratch[3:6, D * g:D * (g + 1), :].rearrange("c p t -> p c t"), B3[:, :, :])\
               .then_inc(rest_stored if g else first_rest, 16)

        MAIN, REST = 6 * 16, 2 * 16

        @block.sync
        def _(sp):
            for b in range(B):
                sp.dma_start(X[:, b], x[b * S:(b + 1) * S].rearrange("(t p) c -> p t c", p=128))\
                  .then_inc(x_loaded[b], 16)
                if b == 0:
                    sp.dma_start(W[:, :], wmat).then_inc(w_loaded, 16)
                    sp.dma_start(C[:, :], wcol).then_inc(w_loaded, 16)
                    sp.dma_start(R[:, :], wrow.to_broadcast([128, R_WIDTH])).then_inc(w_loaded, 16)

            def load_max(p, u):
                for hh in range(2):
                    rows = slice(64 * hh, 64 * hh + MROWS)
                    sp.dma_start(MXQ[rows, u, hh, :], qc[0:3, bass.ds(DH * (2 * p + hh), DH), :]).then_inc(ld_mx[u], 16)
                    sp.dma_start(MXK[rows, u, :], kc[0:3, bass.ds(DH * (2 * p + hh), DH), :]).then_inc(ld_mx[u], 16)

            def load_scores(p, u):
                for hh in range(2):
                    sp.dma_start(STQ[64 * hh:64 * hh + CROWS, u, hh, :], qc[:, bass.ds(DH * (2 * p + hh), DH), :])\
                      .then_inc(ld_st[u], 16)
                    sp.dma_start(STK[64 * hh:64 * hh + CROWS, u, :], kc[:, bass.ds(DH * (2 * p + hh), DH), :])\
                      .then_inc(ld_st[u], 16)
                sp.dma_start(VR[:, u, :], VA[:, bass.ds(p, 1), :]).then_inc(ld_st[u], 16)

            def load_shift(u):
                for hh in range(2):
                    for part in range(2):
                        r = 64 * hh + CROWS + part
                        sp.dma_start(STQ[r:r + 1, u, hh, :], NB[TILES * hh:TILES * (hh + 1), u, part, :])\
                          .then_inc(ld_m[u], 16)

            def store_result(p, u):
                for hh in range(2):
                    for qh in range(2):
                        g = 2 * hh + qh
                        sp.dma_start(os_[bass.ds(2 * p + hh, 1), qh], E[32 * g:32 * g + VROW, u, :])\
                          .then_inc(e_store[u], 16)

            def pair(p, u, first=False, left=3):
                if left >= 1:
                    if not first:
                        sp.wait_ge(pv_done, TILES * p)
                    load_scores(p + 1, 1 - u)
                if not first:
                    sp.wait_ge(evac, p)
                    store_result(p - 1, 1 - u)
                if left >= 3:
                    sp.wait_ge(mx_ready, 2 * TILES * (p + 2))
                    load_max(p + 3, 1 - u)
                if left >= 1:
                    sp.wait_ge(nm_ready, p + 2)
                    load_shift(1 - u)

            sp.wait_ge(fill_ready, 2)
            for kind, part, there in (("k", 0, k_first), ("q", 1, q_second), ("k", 1, k_second)):
                sp.wait_ge(there, 2)
                load_first(sp, kind, part)
            store_main(sp, 0)
            store_main(sp, 0, q=False)
            sp.wait_ge(first_main, MAIN)
            load_max(1, 1)
            sp.wait_ge(fill_ready, 4)
            sp.wait_ge(q_third, 1)
            store_rest(sp, 0)
            sp.wait_ge(k_third, 1)
            store_rest(sp, 0, q=False)
            sp.wait_ge(first_rest, REST)
            sp.wait_ge(v_ready, 2)
            load_scores(0, 0)
            sp.wait_ge(nm_ready, 1)
            load_shift(0)
            sp.wait_ge(mx_ready, 2 * TILES)
            load_max(2, 0)
            pair(0, 0, first=True)
            with sp.Fori(0, 2) as k:
                pair(2 * k + 1, 1)
                pair(2 * k + 2, 0)
            for g in range(SEGMENTS - 1):
                sp.wait_ge(main_stored, MAIN * (g + 1))
                sp.wait_ge(rest_stored, REST * (g + 1))
                sp.wait_ge(v_ready, 2 * (g + 2))
                with sp.Fori(4 * g + 2, 4 * g + 6) as k:
                    pair(2 * k + 1, 1)
                    pair(2 * k + 2, 0)
            sp.wait_ge(wl_zero, 1)
            for hh in range(2):
                for half in range(2):
                    at, head = 32 * (2 * hh + half), DH * (H - 2 + hh)
                    sp.dma_start(WL[at:at + DH, half, hh * OUTW:(hh + 1) * OUTW],
                                 wmat[head:head + DH, W_COLS["p2"][0]:W_COLS["p2"][1]]).then_inc(wl_loaded, 16)
            for left in (2, 1, 0):
                p = ALL_PAIRS - 1 - left
                pair(p, p % 2, left=left)
            sp.wait_ge(on_ready, SEGMENTS - 1)
            for u in range(2):
                sp.wait_ge(e_store[u], 64 * (ALL_PAIRS // 2 - u))
            heads = slice(H * (SEGMENTS - 1), H * SEGMENTS - 2)
            for qh in range(2):
                here = slice(qh * HALF, (qh + 1) * HALF)
                sp.dma_start(DEN[0:LAST, here], os_[heads, qh, DH:VROW, :].to_broadcast([H - 2, DH, HALF]))\
                  .then_inc(last_loaded[qh], 16)
                sp.dma_start(ON[0:LAST, here], os_[heads, qh, 0:DH, :]).then_inc(last_loaded[qh], 16)
            for b in range(B):
                for n in range(2):
                    sp.wait_ge(out_ready, 2 * b + n + 1)
                    at = b * S + n * HALF
                    sp.dma_start(out[at:at + HALF].rearrange("(t p) c -> p t c", p=128), X[:, b, 4 * n:4 * n + 4])\
                      .then_inc(out_stored, 16)
            sp.wait_ge(out_stored, 16 * 2 * B)
            sp.wait_ge(rc_stored, 16 * 3)

        @block.tensor
        def _(pe):
            def maxima(pm, u, qt, it):
                if qt == 0 and isinstance(pm, int) and pm == 0:
                    pe.wait_ge(ld_queries, 4 * 16)
                    pe.wait_ge(ld_first, 8 * 16)
                elif qt == 0:
                    pe.wait_ge(ld_mx[u], 64 * (it + u))
                for hh in range(2):
                    wait(pe, mx_taken, 2 * TILES * pm + 2 * qt + hh - 1)
                    for kh in range(2):
                        here = slice(kh * HALF, (kh + 1) * HALF)
                        last = nc.tensor.matmul(MX[:, hh, here], MXQ[:, u, hh, qt * 128:(qt + 1) * 128],
                                                MXK[:, u, here], start=True, stop=True)
                    last.then_inc(mx_ready, 1)

            def wait_read(tile, turned):
                if tile is None:
                    wait(pe, nm_ready, turned)
                    return
                kind, g, n = tile
                if kind == "t":
                    pe.wait_ge(xnt_ready, 2 * g + n + 1)
                elif kind == "q":
                    pe.wait_ge(q_first, 2 * g + n + 1)
                elif kind == "k":
                    pe.wait_ge(k_rest, 2 * g + n + 1)
                elif kind == "v":
                    pe.wait_ge(v_ready, 2 * g + n + 1)
                elif kind == "n":
                    pe.wait_ge(n_act, g - B + 1)
                elif kind == "r":
                    pe.wait_ge(q_normed, 2 * (g - B) + n + 1)
                elif kind == "y":
                    pe.wait_ge(y_taken, 2 * g + n + 1)
                elif kind == "z":
                    pe.wait_ge(z_taken, n + 1)

            def turn_maxima(pm, u):
                pe.wait_ge(mx_taken, 2 * TILES * pm + 2 * TILES)
                wait_read(last_tile(pm - 1, TURN_STEP, turning=True), pm)
                nc.tensor.transpose(XB[0:2 * TILES, 0:128], NM[:, u, :], w["ident"]).then_inc(xb_full, 1)

            def scores(p, u, s, half):
                for hh in range(2):
                    j = 2 * half + hh
                    n = 4 * TILES * p + 4 * s + j
                    if not wide(p, s):
                        wait(pe, exp_done, n - 1)
                    elif wide(*later(p, s, -1)):
                        pe.wait_ge(exp_done, n - 3)
                    elif j < 2:
                        pe.wait_ge(exp_done, n - 1)
                    nc.tensor.matmul(score_bank(p, s, j), STK[:, u, s * 128:(s + 1) * 128],
                                     STQ[:, u, hh, half * HALF:(half + 1) * HALF],
                                     start=True, stop=True).then_inc(st_ready, 1)

            def values(p, u, s):
                pe.wait_ge(exp_done, 4 * TILES * p + 4 * s + 4)
                if s == 0:
                    wait(pe, evac, p)
                for j in range(4):
                    half, hh = j // 2, j % 2
                    g = 2 * hh + half
                    v = (hh * TILES + s) * VROW
                    last = nc.tensor.matmul(PV[32 * g:32 * g + VROW, :], VR[:, u, v:v + VROW],
                                            PT[:, s % 2, j, :], start=(s == 0), stop=(s == TILES - 1))
                last.then_inc(pv_done, 1)

            def pair(p, u, it, first=False, left=2):
                pe.wait_ge(ld_st[u], 80 * it + 80)
                pe.wait_ge(ld_m[u], 64 * it + 64)
                for s in range(TILES):
                    if s == TURN_STEP and left >= 1:
                        turn_maxima(p + 1, 1 - u)
                    scores(p, u, s, 0)
                    for i, (ahead, qt) in enumerate(due(p, s)):
                        if i == 1:
                            scores(p, u, s, 1)
                        if ahead <= left:
                            maxima(p + ahead, (u + ahead) % 2, qt, it + (u + ahead) // 2)
                    if len(due(p, s)) == 1:
                        scores(p, u, s, 1)
                    if s > 0:
                        values(p, u, s - 1)
                    elif not first:
                        values(p - 1, 1 - u, TILES - 1)
                    for kind, g, n in extra_at(p, s):
                        wait_read(last_tile(p, s), p + 1 + (s >= TURN_STEP))
                        tile(kind, g, n, XB[:, :]).then_inc(xb_full, 1)

            def body(it, first=False, last=False):
                pair(2 * it, 0, it, first, left=1 if last else 2)
                pair(2 * it + 1, 1, it, left=0 if last else 2)

            def tile(kind, g, n, to):
                layer = 1 if g < B else 2
                here = slice(n * HALF, (n + 1) * HALF)
                if kind == "t":
                    if g >= B:
                        pe.wait_ge(xn_ready, 2 * (g - B) + n + 1)
                    for t in range(4):
                        if g < B:
                            pe.wait_ge(xn_first, TILES * g + 4 * n + t + 1)
                        last = nc.tensor.transpose(to[:, t * 128:(t + 1) * 128], XN[:, 4 * n + t, :], w["ident"])
                elif kind in ("q", "k"):
                    pe.wait_ge(xnt_ready, 2 * g + n + 1)
                    last = nc.tensor.matmul(to, w[f"{kind}{layer}"], XNT[:, here], start=True, stop=True)
                elif kind == "v":
                    pe.wait_ge(xnt_ready, 2 * g + n + 1)
                    for t in range(4):
                        k = 4 * n + t
                        last = nc.tensor.matmul(to[:, t * 128:(t + 1) * 128], XNT[:, k * 128:(k + 1) * 128],
                                                w[f"v{layer}"], start=True, stop=True)
                elif kind == "n":
                    pe.wait_ge(sq_act, 2 * (g - B) + 2)
                    for t in range(TILES):
                        last = nc.tensor.matmul(to[:, t * H:(t + 1) * H], SQ[:, t * 128:(t + 1) * 128], w["heads"],
                                                start=True, stop=True)
                elif kind == "r":
                    pe.wait_ge(rn_ready, 2 * (g - B) + n + 1)
                    for t in range(4):
                        k = 4 * n + t
                        last = nc.tensor.matmul(to[:, t * 128:(t + 1) * 128], RH[:, k * D:(k + 1) * D], w["ident"],
                                                start=True, stop=True)
                elif kind == "y":
                    pe.wait_ge(on_ready, g + 1)
                    for t in range(4):
                        k = 4 * n + t
                        last = nc.tensor.matmul(to[:, t * 128:(t + 1) * 128], ONN[:, k * 128:(k + 1) * 128],
                                                w["o1"], start=True, stop=True)
                else:
                    rows = D if g == 0 else LAST
                    if g == 0:
                        pe.wait_ge(on_ready, B + 1)
                    for t in range(3 * n, min(3 * n + 3, TILES)):
                        if g == 1:
                            pe.wait_ge(last_ready, 1 + t // 4)
                        last = nc.tensor.matmul(to[:, t % 3 * OUTW:(t % 3 + 1) * OUTW],
                                                ONN[0:rows, t * 128:(t + 1) * 128], w["p2"][0:rows],
                                                start=True, stop=True)
                return last

            pe.wait_ge(w_loaded, 48)
            pe.wait_ge(scaled, 2)
            for kind, g, n in FIRST[:8]:
                tile(kind, g, n, first_bank[kind, g, n]).then_inc(first_full, 1)
            for qt in range(TILES):
                maxima(0, 0, qt, 0)
                for kind, g, n in BETWEEN.get(qt, []):
                    if kind == "q":
                        pe.wait_ge(v_ready, 2)
                    elif kind == "v":
                        pe.wait_ge((q_first, k_first)[n], 3)
                    tile(kind, g, n, first_bank[kind, g, n]).then_inc(first_full, 1)
            pe.wait_ge(q_first, 4)
            turn_maxima(0, 0)
            for qt in range(FIRST_AHEAD):
                maxima(1, 1, qt, 0)
            pe.wait_ge(v_full, 2)
            pe.wait_ge(k_first, 4)
            pe.wait_ge(pv_zero, 1)
            for lo, hi in SPANS:
                if hi - lo == 1:
                    body(lo, first=lo == 0, last=hi == ITERATIONS)
                else:
                    wait_read(last_tile(2 * lo, 0), 2 * lo + 1)
                    with pe.Fori(lo, hi) as it:
                        body(it)
            pe.wait_ge(z_taken, 3)
            for n in range(3):
                tile("z", 1, n, last_bank[n]).then_inc(z_ready, 1)
                if n == 0:
                    values(ALL_PAIRS - 1, 1, TILES - 1)
            pe.wait_ge(wl_loaded, 64)
            pe.wait_ge(wl_sums, 1)
            pe.wait_ge(evac, ALL_PAIRS)
            for t in range(TILES):
                if t >= 5:
                    pe.wait_ge(z_taken, 3 + t - 4)
                nc.tensor.matmul(pair_bank[t][:, 0:2 * OUTW + 2], E[:, 1, t % 4 * 128:(t % 4 + 1) * 128],
                                 WL[:, t // 4, :], start=True, stop=True).then_inc(pair_ready, 1)

        @block.scalar
        def _(act):
            def pair(p, u, it, first=False):
                for s in range(TILES):
                    step = TILES * p + s
                    for j in range(4):
                        n = 4 * step + j
                        act.wait_ge(st_ready, n + 1)
                        if j == 0:
                            wait(act, pv_done, step - 1)
                        nc.scalar.activation(PT[:, s % 2, j, :], score_bank(p, s, j), ACT.Exp)\
                          .then_inc(exp_done, 1)
                        if s == 1 and j == 1 and not first:
                            copy_out(p, 1 - u, 64 * (it - 1 + u))
                        if j == 1:
                            for name, g, n, use in at_step(act_reads, p, s):
                                act_extra(name, g, n, use)
                    for name, g, n in at_step(act_follow, p, s):
                        act_extra(name, g, n)

            def copy_out(pairs, u, stored):
                act.wait_ge(pv_done, TILES * pairs)
                wait(act, e_store[u], stored)
                nc.scalar.copy(E[:, u, :], PV[:, :]).then_inc(evac, 1)

            def body(it, first=False):
                pair(2 * it, 0, it, first)
                pair(2 * it + 1, 1, it)

            def act_extra(name, g, n, use=None, src=XB[:, :]):
                here = slice(n * HALF, (n + 1) * HALF)
                layer = 1 if g < B else 2
                if use is not None:
                    act.wait_ge(xb_full, use + 1)
                if name == "t":
                    nc.scalar.copy(XNT[:, here], src).then_inc(xnt_ready, 1)
                elif name in ("q", "k"):
                    if n == 0 and g > 1:
                        act.wait_ge(main_stored, MAIN * (g - 1))
                        act.wait_ge(rest_stored, REST * (g - 1))
                    if name == "k":
                        nc.scalar.activation(KB[:, 2, here], src, ACT.Identity, bias=col[f"bk{layer}"])\
                          .then_inc(k_first, 1)
                    elif layer == 1:
                        nc.scalar.activation(QB[:, 0, here], src, ACT.Identity, bias=qbias[:, :])\
                          .then_inc(q_first, 1)
                    else:
                        nc.scalar.activation(QT[:, here], src, ACT.Identity, bias=col["bq2"]).then_inc(q_first, 1)
                elif name == "q second":
                    act.wait_ge(q_rest, 2 * g + n + 1)
                    nc.scalar.copy(QB[:, 1, here], QR[:, here]).then_inc(q_second, 1)
                elif name == "k second":
                    act.wait_ge(k_rest, 2 * g + n + 1)
                    nc.scalar.copy(KB[:, 1, here], KR[:, here]).then_inc(k_second, 1)
                elif name == "squares":
                    act.wait_ge(q_first, 2 * g + n + 1)
                    nc.scalar.activation(SQ[:, here], QT[:, here], ACT.Square).then_inc(sq_act, 1)
                elif name == "n":
                    wait(act, rn_ready, 2 * (g - B))
                    nc.scalar.copy(N2[:, :], src[:, 0:TILES * H]).then_inc(n_act, 1)
                elif name == "gates":
                    gates(g)

            def gates(b):
                act.wait_ge(g_dve, G_STEPS * b + G_BEFORE)
                nc.scalar.activation(GE[:, :, :], GL[:, :, :], ACT.Exp).then_inc(g_act, 1)

            act.wait_ge(w_loaded, 48)
            nc.scalar.activation(qbias[:, :], col["bq1"], ACT.Identity, scale=DH ** -0.5).then_inc(scaled, 1)
            act.wait_ge(scaled, 2)

            def norm(g):
                act.wait_ge(x_loaded[g], 16)
                act.wait_ge(ln_pool, 2 * g + 2)
                for t in range(TILES):
                    nc.scalar.activation(XN[:, t, :], X[:, g, t, :], ACT.Identity, bias=shift[:, t:t + 1],
                                         scale=rstd[:, t:t + 1]).then_inc(xn_first, 1)

            norm(0)
            for full, (kind, g, n) in enumerate(FIRST[:6]):
                act.wait_ge(first_full, full + 1)
                act_extra(kind, g, n, src=first_bank[kind, g, n])
                if (kind, n) == ("k", 0):
                    act_extra("q second", 0, 0)
            for name, n in (("k second", 0), ("q second", 1), ("k second", 1)):
                act_extra(name, 0, n)
            act.wait_ge(small_ready, 2)
            nc.scalar.activation(soft[:, 1:2], soft[:, 0:1], ACT.Exp, scale=-1.0).then_inc(small_act, 1)
            act.wait_ge(small_act, 1)
            nc.scalar.activation(soft[:, 2:3], soft[:, 1:2], ACT.Ln, bias=1.0).then_inc(small_act, 1)
            norm(1)
            act.wait_ge(first_full, 8)
            for full, (kind, g, n) in enumerate(FIRST):
                if g == 0:
                    continue
                act.wait_ge(first_full, full + 1)
                src = first_bank[kind, g, n]
                here = slice(n * HALF, (n + 1) * HALF)
                if kind == "q":
                    nc.scalar.activation(QT[:, here], src, ACT.Identity, bias=qbias[:, :]).then_inc(q_full, 1)
                elif kind == "k":
                    nc.scalar.activation(KT[:, here], src, ACT.Identity, bias=col["bk1"]).then_inc(k_full, 1)
                elif kind == "v":
                    nc.scalar.copy(VT[:, here], src).then_inc(v_full, 1)
                if (kind, n) == ("q", 0):
                    act.wait_ge(first_main, MAIN)
                    act.wait_ge(first_rest, REST)
                if kind != "v":
                    act_extra(kind, g, n, src=src)
            for name in ("q second", "k second"):
                for n in range(2):
                    act_extra(name, 1, n)
            act_reads, act_follow = {}, {}
            for (p, s), (kind, g, n) in sorted(EXTRA.items()):
                if kind in ("t", "q", "k", "n"):
                    act_reads.setdefault(later(p, s, 1), []).append((kind, g, n, xb_use(p, s)))
                if kind == "k":
                    act_follow.setdefault(later(p, s, 2), []).append(("k second", g, n))
                if kind == "q":
                    act_follow.setdefault(later(p, s, 1), []).append(("squares", g, n))
                if kind == "z" and n == 2:
                    act_follow.setdefault(later(p, s, 2), []).append(("gates", g, n))
            for lo, hi in SPANS:
                if hi - lo == 1:
                    body(lo, first=lo == 0)
                else:
                    with act.Fori(lo, hi) as it:
                        body(it)
            copy_out(ALL_PAIRS, 1, 64 * (ALL_PAIRS // 2 - 1))
            gates(1)

        @block.vector
        def _(dve):
            def maximum(pm, u, qt):
                for hh in range(2):
                    dve.wait_ge(mx_ready, 2 * TILES * pm + 2 * qt + hh + 1)
                    c = hh * TILES + qt
                    nc.vector.tensor_reduce(NM[:, u, c:c + 1], MX[:, hh, :], AX.X, ALU.max, negate=True)\
                      .then_inc(mx_taken, 1)

            def split_maxima(pm, u, stored, use):
                dve.wait_ge(xb_full, use + 1)
                wait(dve, ld_m[u], stored)
                nc.vector.tensor_copy(NB[:, u, 0, :], XB[0:2 * TILES, 0:128]).then_inc(nm_first, 1)
                dve.wait_ge(nm_first, pm + 1)
                nc.vector.tensor_tensor(NB[:, u, 1, :], XB[0:2 * TILES, 0:128], NB[:, u, 0, :], ALU.subtract)\
                  .then_inc(nm_ready, 1)

            def pair(p, u, it, extras, left=2):
                for s in range(TILES):
                    if s == TURN_STEP and left >= 1:
                        split_maxima(p + 1, 1 - u, 64 * (it + u), p + 1 + extras)
                    for ahead, qt in due(p, s):
                        if ahead <= left:
                            maximum(p + ahead, (u + ahead) % 2, qt)
                    for kind, g, n in at_step(norm_steps, p, s):
                        if kind == "stats":
                            token_stats(g, g % B, n)
                        else:
                            norm(g)
                    if s == SUMS_STEP and isinstance(p, int) and p in SUMS_AT:
                        reciprocals(SUMS_AT.index(p))
                    extras += len(extra_at(p, s))
                    for kind, g, n, use in at_step(dve_reads, p, s):
                        dve_extra(kind, g, n, XB[:, :], use)
                        if kind == "z" and n == 2:
                            gates(0)

            def body(it, extras, last=False):
                pair(2 * it, 0, it, extras, left=1 if last else 2)
                if isinstance(it, int):
                    extras = extras_before(2 * it + 1)
                pair(2 * it + 1, 1, it, extras, left=0 if last else 2)

            def dve_extra(kind, g, n, src, use=None):
                layer = 1 if g < B else 2
                here = slice(n * HALF, (n + 1) * HALF)
                if kind in ("q", "k"):
                    dve.wait_ge(q_first if kind == "q" else k_first, 2 * g + n + 1)
                    rest, part = (QR, QB[:, 0, here]) if kind == "q" else (KR, KB[:, 2, here])
                    bias = qbias[:, :] if kind == "q" else col[f"bk{layer}"]
                    nc.vector.scalar_tensor_tensor(rest[:, here], src, bias, part, ALU.add, ALU.subtract)\
                      .then_inc(q_rest if kind == "q" else k_rest, 1)
                    return
                if use is not None:
                    dve.wait_ge(xb_full, use + 1)
                if kind == "v":
                    for t in range(4):
                        last = nc.vector.tensor_tensor(
                            values_of(g, 4 * n + t), src[:, t * 128:(t + 1) * 128].rearrange("p (h d) -> p h d", d=DH),
                            row[f"bv{layer}"].rearrange("p (h d) -> p h d", d=DH), ALU.add)
                    last.then_inc(v_ready, 1)
                elif kind == "y":
                    dve.wait_ge(biased, g + 1)
                    Xh = X[:, g, 4 * n:4 * n + 4, :].rearrange("p t c -> p (t c)")
                    nc.vector.tensor_tensor(Xh, src, Xh, ALU.add).then_inc(y_taken, 1)
                elif kind == "r":
                    nc.vector.tensor_tensor(QT[:, here], src, QT[:, here], ALU.mult).then_inc(q_normed, 1)
                elif kind == "z":
                    take_z(n, src)

            def take_z(n, src):
                m = min(3, TILES - 3 * n)
                return nc.vector.tensor_copy(Z[:, 3 * n:3 * n + m, :],
                                             src[:, 0:m * OUTW].rearrange("p (t c) -> p t c", t=m))\
                         .then_inc(z_taken, 1)

            def token_stats(g, b, n):
                if g >= B:
                    dve.wait_ge(y_taken, 2 * b + n + 1)
                for t in range(4 * n, 4 * n + 4):
                    last = nc.vector.bn_stats(stats[:, t, :], X[:, b, t, :])
                last.then_inc(stats_dve, 1)

            def norm(g):
                wait(dve, ln_pool, 2 * g)
                dve.wait_ge(stats_dve, 3 * g + 2)
                for t in range(TILES):
                    last = nc.vector.bn_aggr(mv[:, t, :], stats[:, t, :])
                last.then_inc(stats_dve, 1)
                dve.wait_ge(stats_dve, 3 * g + 3)
                nc.vector.tensor_scalar(var[:, :], mv[:, :, 1], EPS, None, ALU.add).then_inc(var_ready, 1)
                nc.vector.tensor_scalar(neg_mean[:, :], mv[:, :, 0], -1.0, None, ALU.mult).then_inc(var_ready, 1)

            def reciprocals(e):
                dve.wait_ge(dc_loaded, 16 * e + 16)
                nc.vector.reciprocal(RC[:, :], DC[:, :]).then_inc(dc_ready, 1)

            def gates(b):
                steps = [0]

                def then(ins):
                    steps[0] += 1
                    ins.then_inc(g_dve, 1)
                    dve.wait_ge(g_dve, G_STEPS * b + steps[0])

                if b == 0:
                    dve.wait_ge(z_taken, 3)
                else:
                    dve.wait_ge(pair_added, 2 * TILES)
                then(nc.vector.tensor_tensor(GL[:, :, :], Z[:, :, D:OUTW],
                                             row["brs"].unsqueeze(1).to_broadcast([128, TILES, NG + 2]), ALU.add))
                part = [slice(0, NG), slice(NG, NG + 2)]
                for i in range(2):
                    then(nc.vector.tensor_reduce(GM[:, i, :], GL[:, :, part[i]], AX.X, ALU.max))
                for i in range(2):
                    n = part[i].stop - part[i].start
                    then(nc.vector.tensor_tensor(GL[:, :, part[i]], GL[:, :, part[i]],
                                                 GM[:, i, :].unsqueeze(2).to_broadcast([128, TILES, n]),
                                                 ALU.subtract))
                assert steps[0] == G_BEFORE
                dve.wait_ge(g_act, b + 1)
                for t in range(TILES):
                    last = nc.vector.max(T8[:, t, :], GE[:, t, 0:NG])
                then(last)
                for i in range(2):
                    then(nc.vector.tensor_reduce(GS[:, i, :], GE[:, :, part[i]], AX.X, ALU.add))
                then(nc.vector.reciprocal(GR[:, :, :], GS[:, :, :]))
                then(nc.vector.tensor_reduce(G3[:, 0, :], T8[:, :, 0:TOP], AX.X, ALU.add))
                then(nc.vector.tensor_tensor(G3[:, 0, :], G3[:, 0, :], GR[:, 0, :], ALU.mult))
                then(nc.vector.tensor_tensor(SW[:, :, :], GE[:, :, part[1]],
                                             GR[:, 1, :].unsqueeze(2).to_broadcast([128, TILES, 2]), ALU.mult))
                then(nc.vector.tensor_tensor(G3[:, 1, :], SW[:, :, 0], SW[:, :, 1], ALU.add))
                then(nc.vector.tensor_tensor(G3[:, 1, :], G3[:, 1, :], SW[:, :, 0], ALU.mult))
                then(nc.vector.tensor_tensor(G3[:, 2, :], G3[:, 0, :], SW[:, :, 1], ALU.mult))
                then(nc.vector.tensor_scalar(G3[:, 1, :], G3[:, 1, :], 2.0, None, ALU.mult))
                then(nc.vector.tensor_scalar(G3[:, 2, :], G3[:, 2, :], 2.0 * TOP, None, ALU.mult))
                then(nc.vector.tensor_tensor(gate[:, :], G3[:, 1, :], G3[:, 2, :], ALU.add))
                dve.wait_ge(biased, B + b + 1)
                for t in range(TILES):
                    last = nc.vector.scalar_tensor_tensor(X[:, b, t, :], Z[:, t, 0:D], gate[:, t:t + 1],
                                                          X[:, b, t, :], ALU.mult, ALU.add)
                    if t % 4 == 3:
                        last.then_inc(out_ready, 1)
                assert steps[0] == G_STEPS, steps[0]

            for tile in (MXQ, MXK):
                nc.vector.memset(tile[:].bitcast(F32), 0.0).then_inc(fill_ready, 1)
            nc.vector.memset(half_neg[:, :], -0.5).then_inc(small_ready, 1)
            dve.wait_ge(x_loaded[0], 16)
            for n in range(2):
                token_stats(0, 0, n)
            norm(0)
            nc.vector.memset(STK[:, :, :], 1.0).then_inc(fill_ready, 1)
            dve.wait_ge(w_loaded, 48)
            nc.vector.tensor_scalar(w["q1"], w["q1"], DH ** -0.5, None, ALU.mult).then_inc(scaled, 1)
            dve.wait_ge(scaled, 2)
            nc.vector.scalar_tensor_tensor(soft[:, 0:1], col["temp"], -1.0, col["temp"], ALU.mult, ALU.max)\
              .then_inc(small_ready, 1)
            for kind, g, n in FIRST[2:6]:
                dve_extra(kind, g, n, first_bank[kind, g, n])
            dve.wait_ge(ones_ready, 1)
            for full in (6, 7):
                kind, g, n = FIRST[full]
                dve.wait_ge(first_full, full + 1)
                dve_extra(kind, g, n, first_bank[kind, g, n])
            nc.vector.memset(STQ[:].bitcast(F32), 0.0).then_inc(fill_ready, 1)
            nc.vector.memset(WL[:, :, 0:2 * OUTW], 0.0).then_inc(wl_zero, 1)
            nc.vector.tensor_copy(WL[:, :, 2 * OUTW:], w["sums"].rearrange("p (a h) -> p a h", a=2)).then_inc(wl_sums, 1)
            dve.wait_ge(x_loaded[1], 16)
            for n in range(2):
                token_stats(1, 1, n)
            norm(1)
            for qt in range(TILES):
                maximum(0, 0, qt)
            split_maxima(0, 0, 0, 0)
            dve.wait_ge(v_full, 1)
            nc.vector.memset(PV[:, :], 0.0).then_inc(pv_zero, 1)
            for qt in range(FIRST_AHEAD):
                maximum(1, 1, qt)
            dve.wait_ge(small_act, 2)
            nc.vector.scalar_tensor_tensor(head_scale[:, :], col["temp"], 0.0, soft[:, 2:3], ALU.max, ALU.add)\
              .then_inc(small_ready, 1)
            dve.wait_ge(small_ready, 3)
            nc.vector.tensor_scalar(head_scale[:, :], head_scale[:, :], DH ** -0.5, None, ALU.mult)\
              .then_inc(small_ready, 1)
            dve_reads = {}
            for (p, s), (kind, g, n) in sorted(EXTRA.items()):
                if kind in ("v", "y", "z", "r"):
                    dve_reads.setdefault((p, s), []).append((kind, g, n, xb_use(p, s)))
                elif kind == "k":
                    dve_reads.setdefault(later(p, s, 1), []).append((kind, g, n, xb_use(p, s)))
            norm_steps = {}
            for (p, s), (kind, g, n) in EXTRA.items():
                if kind == "y":
                    norm_steps.setdefault(later(p, s, 1), []).append(("stats", g + B, n))
                if kind == "y" and n == 1:
                    norm_steps.setdefault(later(p, s, 3), []).append(("norm", g + B, n))
            for lo, hi in SPANS:
                extras = extras_before(2 * lo)
                if hi - lo == 1:
                    body(lo, extras, last=hi == ITERATIONS)
                else:
                    with dve.Fori(lo, hi) as it:
                        body(it, extras)
            for half in range(2):
                here = slice(half * HALF, (half + 1) * HALF)
                dve.wait_ge(last_loaded[half], 32)
                nc.vector.reciprocal(RDEN[0:LAST, here], DEN[0:LAST, here]).then_inc(last_inverse, 1)
                dve.wait_ge(last_inverse, half + 1)
                nc.vector.tensor_tensor(ONN[0:LAST, here], ON[0:LAST, here], RDEN[0:LAST, here], ALU.mult)\
                  .then_inc(last_ready, 1)
            for n in range(3):
                dve.wait_ge(z_ready, n + 1)
                take_z(n, last_bank[n])
            dve.wait_ge(z_taken, 6)
            for i in range(TILES + 2):
                if i < TILES:
                    dve.wait_ge(pair_ready, i + 1)
                    nc.vector.reciprocal(RS[:, i, :], pair_bank[i][:, 2 * OUTW:2 * OUTW + 2]).then_inc(rs_ready, 1)
                for hh in range(2):
                    t = i - 1 - hh
                    if not 0 <= t < TILES:
                        continue
                    if hh == 0:
                        dve.wait_ge(rs_ready, t + 1)
                    else:
                        dve.wait_ge(pair_added, max(1, 2 * t))
                    nc.vector.scalar_tensor_tensor(Z[:, t, :], pair_bank[t][:, hh * OUTW:(hh + 1) * OUTW],
                                                   RS[:, t, hh:hh + 1], Z[:, t, :], ALU.mult, ALU.add)\
                      .then_inc(pair_added, 1)
            gates(1)

        @block.gpsimd
        def _(pool):
            nc.gpsimd.memset(VA[:, :, :], 1.0).then_inc(ones_ready, 1)

            def norm(g, b):
                pool.wait_ge(var_ready, 2 * g + 1)
                if 0 < g <= B:
                    pool.wait_ge(xn_first, TILES * g)
                elif g > B:
                    pool.wait_ge(xn_ready, 2 * (g - B))
                nc.gpsimd.tensor_tensor(rstd[:, :], var[:, :], half_neg[:, 0:TILES], ALU.pow).then_inc(ln_pool, 1)
                pool.wait_ge(ln_pool, 2 * g + 1)
                pool.wait_ge(var_ready, 2 * g + 2)
                nc.gpsimd.tensor_tensor(shift[:, :], neg_mean[:, :], rstd[:, :], ALU.mult).then_inc(ln_pool, 1)
                if g < B:
                    return
                pool.wait_ge(ln_pool, 2 * g + 2)
                wait(pool, xnt_ready, 2 * g)
                for t in range(TILES):
                    last = nc.gpsimd.tensor_scalar(XN[:, t, :], X[:, b, t, :], rstd[:, t:t + 1],
                                                   shift[:, t:t + 1], ALU.mult, ALU.add)
                    if t % 4 == 3:
                        last.then_inc(xn_ready, 1)

            def third(g, layer):
                if layer == 1:
                    pool.wait_ge(q_second, 2 * g + 2)
                    nc.gpsimd.tensor_tensor(QB[:, 2, :], QR[:, :], QB[:, 1, :], ALU.subtract).then_inc(q_third, 1)
                pool.wait_ge(k_second, 2 * g + 2)
                nc.gpsimd.tensor_tensor(KB[:, 0, :], KR[:, :], KB[:, 1, :], ALU.subtract).then_inc(k_third, 1)

            def store(g, q):
                store_main(pool, g, q)
                store_rest(pool, g, q)

            def queries2(g):
                k = [6 * (g - B)]

                def then(ins):
                    k[0] += 1
                    ins.then_inc(q_pool, 1)
                    pool.wait_ge(q_pool, k[0])

                pool.wait_ge(n_act, g - B + 1)
                for half in range(2):
                    few = slice(half * TILES * H // 2, (half + 1) * TILES * H // 2)
                    then(nc.gpsimd.tensor_tensor(RN[:, few], N2[:, few], half_neg[:, few], ALU.pow))
                    nc.gpsimd.tensor_scalar(RH[:, half * HALF:(half + 1) * HALF].rearrange("p (k d) -> p k d", d=DH),
                                            RN[:, few].unsqueeze(2).to_broadcast([128, TILES * H // 2, DH]),
                                            1.0, 1.0, ALU.mult, ALU.mult).then_inc(rn_ready, 1)
                pool.wait_ge(q_normed, 2 * (g - B) + 2)
                pool.wait_ge(small_ready, 4)
                then(nc.gpsimd.tensor_scalar(QT[:, :], QT[:, :], col["qe"], head_scale[:, :], ALU.add, ALU.mult))
                then(nc.gpsimd.tensor_scalar(QB[:, 0, :], QT[:, :], 1.0, 1.0, ALU.mult, ALU.mult))
                then(nc.gpsimd.tensor_tensor(QR[:, :], QT[:, :], QB[:, 0, :], ALU.subtract))
                then(nc.gpsimd.tensor_scalar(QB[:, 1, :], QR[:, :], 1.0, 1.0, ALU.mult, ALU.mult))
                nc.gpsimd.tensor_tensor(QB[:, 2, :], QR[:, :], QB[:, 1, :], ALU.subtract).then_inc(q_third, 1)
                pool.wait_ge(q_third, g + 1)

            def add_bias(b, layer):
                if layer == 1:
                    pool.wait_ge(xn_first, TILES * (b + 1))
                else:
                    pool.wait_ge(xn_ready, 2 * (b + 1))
                nc.gpsimd.tensor_tensor(X[:, b], X[:, b], row["bo1" if layer == 1 else "bp"].unsqueeze(1)
                                        .to_broadcast([128, TILES, D]), ALU.add).then_inc(biased, 1)

            def reload(e):
                for u in range(2):
                    pool.wait_ge(e_store[u], 256 * e + 256)
                wait(pool, on_ready, e)
                for qh in range(2):
                    here = slice(qh * HALF, (qh + 1) * HALF)
                    src = os_[H * e:H * (e + 1), qh]
                    pool.dma_start(ON[:, here], src[:, 0:DH, :]).then_inc(on_loaded, 16)

            def divide(e):
                heads = slice(H * e, H * (e + 1))
                pool.dma_start(DC[:, :], os_[heads, :, DH, :].rearrange("h a (k n) -> (h a) k n", n=128))\
                    .then_inc(dc_loaded, 16)
                pool.wait_ge(dc_ready, e + 1)
                pool.dma_start(rs_[heads].rearrange("h (k n) -> (h k) n", n=128), RC[:, :]).then_inc(rc_stored, 16)
                pool.wait_ge(rc_stored, 16 * e + 16)
                pool.dma_start(RDEN[:, :], rs_[heads].unsqueeze(1).to_broadcast([H, DH, S])).then_inc(r_loaded, 16)
                pool.wait_ge(r_loaded, 16 * e + 16)
                pool.wait_ge(on_loaded, 32 * e + 32)
                nc.gpsimd.tensor_tensor(ONN[:, :], ON[:, :], RDEN[:, :], ALU.mult).then_inc(on_ready, 1)

            norm(0, 0)
            pool.wait_ge(fill_ready, 2)
            pool.wait_ge(q_first, 2)
            load_first(pool, "q", 0)
            pool.wait_ge(w_loaded, 48)
            third(0, 1)
            norm(1, 1)
            for full, first, whole, B3, slot, rest, done in ((q_full, q_first, QT, QB, 0, QR, q_rest),
                                                             (k_full, k_first, KT, KB, 2, KR, k_rest)):
                for n in range(2):
                    here = slice(n * HALF, (n + 1) * HALF)
                    pool.wait_ge(full, n + 1)
                    pool.wait_ge(first, 2 + n + 1)
                    nc.gpsimd.tensor_tensor(rest[:, here], whole[:, here], B3[:, slot, here], ALU.subtract)\
                      .then_inc(done, 1)
            for n in range(2):
                pool.wait_ge(v_full, n + 1)
                for t in range(4 * n, 4 * n + 4):
                    last = nc.gpsimd.tensor_tensor(values_of(1, t), VT[:, t * 128:(t + 1) * 128]
                                                   .rearrange("p (h d) -> p h d", d=DH),
                                                   row["bv1"].rearrange("p (h d) -> p h d", d=DH), ALU.add)
                last.then_inc(v_ready, 1)
            for b in range(B):
                add_bias(b, 1)
            third(1, 1)
            pool.wait_ge(q_third, 2)
            store(1, True)
            pool.wait_ge(k_third, 2)
            store(1, False)
            for b in range(B):
                reload(b)
                divide(b)
                norm(B + b, b)
                add_bias(b, 2)
                queries2(B + b)
                store(B + b, True)
                third(B + b, 2)
                pool.wait_ge(k_third, B + b + 1)
                store(B + b, False)
            reload(2)
            divide(2)


_INS = ["x", "wmat", "wcol", "wrow"]


def kernel(**inputs):
    import numpy as np
    import concourse.bacc as bacc
    from concourse.bass_utils import run_bass_kernel_spmd

    a = {n: np.asarray(v) for n, v in inputs.items()}
    L1 = {n: a["L0_attn_" + n] for n in ("x", "Wq", "bq", "Wk", "bk", "Wv", "bv", "Wo", "bo")}
    L2 = {n: a["L0_ffn_" + n] for n in ("Wq", "bq", "Wk", "bk", "Wv", "bv", "Wp", "bp", "Wr", "br", "Ws", "bs",
                                         "temperature", "query_embedding")}
    f = np.float32
    eye = np.eye(D, dtype=f)
    heads = np.kron(np.eye(H, dtype=f), np.ones((DH, 1), f))
    sums = np.zeros((D, 2, 2), f)
    for hh in range(2):
        for half in range(2):
            sums[32 * (2 * hh + half) + DH, half, hh] = 1
    arrays = {
        "x": np.ascontiguousarray(L1["x"].reshape(B * S, D)),
        "wmat": np.ascontiguousarray(np.concatenate(
            [L1["Wq"].T, L1["Wk"].T, L1["Wv"].T, L1["Wo"].T, L2["Wq"].T, L2["Wk"].T, L2["Wv"].T,
             L2["Wp"].T, L2["Wr"].T, L2["Ws"].T, eye, heads, sums.reshape(D, 4)], axis=1)),
        "wcol": np.ascontiguousarray(np.stack(
            [L1["bq"], L1["bk"], L2["bq"], L2["bk"], L2["query_embedding"].reshape(D),
             np.repeat(L2["temperature"].reshape(H), DH)], axis=1)),
        "wrow": np.ascontiguousarray(np.concatenate(
            [L1["bv"], L1["bo"], L2["bv"], L2["bp"], L2["br"], L2["bs"]]).reshape(1, R_WIDTH)),
    }
    nc = bacc.Bacc("TRN2", target_bir_lowering=False, num_devices=1)
    args = [nc.dram_tensor(n, arrays[n].shape, F32, kind="ExternalInput").ap() for n in _INS]
    args.append(nc.dram_tensor("out", (B * S, D), F32, kind="ExternalOutput").ap())
    args.append(nc.dram_tensor("q_parts", (COMBOS, SEGMENTS * D, S), BF16).ap())
    args.append(nc.dram_tensor("k_parts", (COMBOS, SEGMENTS * D, S), BF16).ap())
    args.append(nc.dram_tensor("head_sums", (SEGMENTS * H, 2, VROW, HALF), F32).ap())
    args.append(nc.dram_tensor("reciprocals", (SEGMENTS * H, S), F32).ap())
    moe_attention_program(nc, *args)
    r = run_bass_kernel_spmd(nc, [arrays], core_ids=[0])
    return np.asarray(r.results[0]["out"]).reshape(B, S, D)
```
